# Optimizing a Trainium2 kernel written in Bass

```python
import numpy as np
import jax
import jax.numpy as jnp

def _softmax(x, axis=-1):
    return jax.nn.softmax(x, axis=axis)

def _gelu(x):
    return jax.nn.gelu(x, approximate=True)

def _silu(x):
    return jax.nn.silu(x)

def _sigmoid(x):
    return jax.nn.sigmoid(x)

def _layernorm(x, axis=-1, eps=1e-05):
    m = jnp.mean(x, axis=axis, keepdims=True)
    v = jnp.var(x, axis=axis, keepdims=True)
    return (x - m) / jnp.sqrt(v + eps)

def _scatter_add(tgt, idx, src, axis=0):
    return tgt.at[idx].add(src)

def _segment_sum(src, seg, n):
    return jax.ops.segment_sum(src, seg, n)
kernel_name = 'mk_adaln_d2_jaxref_r8_74970d'

def setup_inputs(seed: int=0):
    np.random.seed(seed)
    _w = jnp.asarray

    def _L0_attn_setup():
        import jax, jax.numpy as jnp
        import numpy as np
        B, S, D, H = (2, 256, 128, 16)
        HD = D // H
        FF = 512
        NUM_ITERS = 8
        DT = 0.1
        LN_EPS = 1e-05

        def _ln(x, g, b):
            m = jnp.mean(x, axis=-1, keepdims=True)
            v = jnp.var(x, axis=-1, keepdims=True)
            return (x - m) * jax.lax.rsqrt(v + LN_EPS) * g + b

        def _forward(x, qkv_w, qkv_b, out_w, out_b, g_attn, b_attn, g1, b1, g2, b2, w_ctx, w_x, b_inl, ff_w1, ff_b1, ff_w2, ff_b2):
            b, s, d = x.shape
            xn = _ln(x, g_attn, b_attn)
            qkv = (xn @ qkv_w + qkv_b).reshape(b, s, 3, H, HD)
            qkv = jnp.transpose(qkv, (2, 0, 3, 1, 4))
            q, k, v = (qkv[0], qkv[1], qkv[2])
            scores = jnp.einsum('bhqd,bhkd->bhqk', q, k) / np.sqrt(HD).astype(np.float32)
            causal = jnp.triu(jnp.ones((s, s), dtype=bool), 1)
            scores = jnp.where(causal[None, None], -jnp.inf, scores)
            attn_w = jax.nn.softmax(scores, axis=-1)
            attn = jnp.einsum('bhqk,bhkd->bhqd', attn_w, v)
            attn = jnp.transpose(attn, (0, 2, 1, 3)).reshape(b, s, d)
            attn = attn @ out_w + out_b
            x = x + attn
            ctx = attn.reshape(b * s, d)
            xs = _ln(x, g1, b1).reshape(b * s, d)
            vs = jnp.zeros_like(xs)

            def step(carry, _):
                xs, vs = carry
                u = jnp.tanh(ctx @ w_ctx + xs @ w_x + b_inl)
                vn = vs + DT * (u - xs - vs)
                xn_ = xs + DT * vn
                return ((xn_, vn), None)
            (xs, vs), _ = jax.lax.scan(step, (xs, vs), None, length=NUM_ITERS)
            x = x + xs.reshape(b, s, d)
            h = _ln(x, g2, b2)
            h = jax.nn.gelu(h @ ff_w1 + ff_b1, approximate=False)
            x = x + (h @ ff_w2 + ff_b2)
            return x
        key = jax.random.key(seed)
        ks = jax.random.split(key, 16)

        def xav(k, shape):
            lim = np.sqrt(6.0 / (shape[0] + shape[1]))
            return jax.random.uniform(k, shape, minval=-lim, maxval=lim, dtype=jnp.float32)
        return {'x': jax.random.normal(ks[0], (B, S, D), dtype=jnp.float32), 'qkv_w': xav(ks[1], (D, 3 * D)), 'qkv_b': jnp.zeros((3 * D,), jnp.float32), 'out_w': xav(ks[2], (D, D)), 'out_b': jnp.zeros((D,), jnp.float32), 'g_attn': jnp.ones((D,), jnp.float32), 'b_attn': jnp.zeros((D,), jnp.float32), 'g1': jnp.ones((D,), jnp.float32), 'b1': jnp.zeros((D,), jnp.float32), 'g2': jnp.ones((D,), jnp.float32), 'b2': jnp.zeros((D,), jnp.float32), 'w_ctx': xav(ks[3], (D, D)), 'w_x': xav(ks[4], (D, D)), 'b_inl': jnp.zeros((D,), jnp.float32), 'ff_w1': xav(ks[5], (D, FF)), 'ff_b1': jnp.zeros((FF,), jnp.float32), 'ff_w2': xav(ks[6], (FF, D)), 'ff_b2': jnp.zeros((D,), jnp.float32)}
    _L0_attn_in = _L0_attn_setup()

    def _L0_ffn_setup():
        import jax, jax.numpy as jnp
        import numpy as np
        B, T, C, H, E = (1, 32, 128, 256, 8)
        STD = 0.02
        key = jax.random.key(seed)
        ks = jax.random.split(key, 8)
        f32 = jnp.float32
        return {'x': jax.random.normal(ks[0], (B, T, C), f32), 'up': jax.random.normal(ks[1], (E, H, C), f32) * STD, 'gate': jax.random.normal(ks[2], (E, H, C), f32) * STD, 'down': jax.random.normal(ks[3], (E, C, H), f32) * STD, 'router': jax.random.normal(ks[4], (E, C), f32) * STD, 'w_up_s': jax.random.normal(ks[5], (H, C), f32) * STD, 'w_gate_s': jax.random.normal(ks[6], (H, C), f32) * STD, 'w_down_s': jax.random.normal(ks[7], (C, H), f32) * STD}
    _L0_ffn_in = _L0_ffn_setup()
    _L0_c = _w((lambda *s: np.random.randn(*s).astype(np.float32) * 0.05)(16, 128))
    _L0_wmod = _w((lambda *s: np.random.randn(*s).astype(np.float32) * 0.05)(128, 6 * 128) * 128 ** (-0.5))

    def _L1_attn_setup():
        import jax, jax.numpy as jnp
        import numpy as np
        B, T, D_MODEL = (2, 128, 128)
        H, DEPTH = (8, 5)
        DH = D_MODEL // H
        key = jax.random.key(seed)
        k_x, k_wp, k_bp, k_wv, k_wo = jax.random.split(key, 5)
        x = jax.random.normal(k_x, (B, T, D_MODEL), dtype=jnp.float32)
        Wp = jax.random.normal(k_wp, (D_MODEL, H * DEPTH), dtype=jnp.float32) * 0.02
        bp = jnp.zeros((H * DEPTH,), dtype=jnp.float32)
        Wv = jax.random.normal(k_wv, (D_MODEL, D_MODEL), dtype=jnp.float32) * 0.02
        Wo = jax.random.normal(k_wo, (D_MODEL, D_MODEL), dtype=jnp.float32) * 0.02
        return {'x': x, 'Wp': Wp, 'bp': bp, 'Wv': Wv, 'Wo': Wo}
    _L1_attn_in = _L1_attn_setup()

    def _L1_ffn_setup():
        import jax, jax.numpy as jnp
        import numpy as np
        ALPHA = 2.0
        TOP_K = 2
        key = jax.random.key(seed)
        ks = jax.random.split(key, 8)
        B, S, D, H, E = (2, 256, 128, 512, 8)
        Er = E - 1
        s_in = 1.0 / np.sqrt(D)
        s_hid = 1.0 / np.sqrt(H)
        return {'x': jax.random.normal(ks[0], (B, S, D), dtype=jnp.float32), 'router_w': jax.random.normal(ks[1], (D, E), dtype=jnp.float32) * s_in, 'up_w': jax.random.normal(ks[2], (Er, D, H), dtype=jnp.float32) * s_in, 'gate_w': jax.random.normal(ks[3], (Er, D, H), dtype=jnp.float32) * s_in, 'down_w': jax.random.normal(ks[4], (Er, H, D), dtype=jnp.float32) * s_hid * 0.1, 'shared_up_w': jax.random.normal(ks[5], (D, H), dtype=jnp.float32) * s_in, 'shared_gate_w': jax.random.normal(ks[6], (D, H), dtype=jnp.float32) * s_in, 'shared_down_w': jax.random.normal(ks[7], (H, D), dtype=jnp.float32) * s_hid * 0.1}
    _L1_ffn_in = _L1_ffn_setup()
    _L1_c = _w((lambda *s: np.random.randn(*s).astype(np.float32) * 0.05)(16, 128))
    _L1_wmod = _w((lambda *s: np.random.randn(*s).astype(np.float32) * 0.05)(128, 6 * 128) * 128 ** (-0.5))
    _d = {'L0_attn_x': _L0_attn_in['x'], 'L0_attn_qkv_w': _L0_attn_in['qkv_w'], 'L0_attn_qkv_b': _L0_attn_in['qkv_b'], 'L0_attn_out_w': _L0_attn_in['out_w'], 'L0_attn_out_b': _L0_attn_in['out_b'], 'L0_attn_g_attn': _L0_attn_in['g_attn'], 'L0_attn_b_attn': _L0_attn_in['b_attn'], 'L0_attn_g1': _L0_attn_in['g1'], 'L0_attn_b1': _L0_attn_in['b1'], 'L0_attn_g2': _L0_attn_in['g2'], 'L0_attn_b2': _L0_attn_in['b2'], 'L0_attn_w_ctx': _L0_attn_in['w_ctx'], 'L0_attn_w_x': _L0_attn_in['w_x'], 'L0_attn_b_inl': _L0_attn_in['b_inl'], 'L0_attn_ff_w1': _L0_attn_in['ff_w1'], 'L0_attn_ff_b1': _L0_attn_in['ff_b1'], 'L0_attn_ff_w2': _L0_attn_in['ff_w2'], 'L0_attn_ff_b2': _L0_attn_in['ff_b2'], 'L0_ffn_up': _L0_ffn_in['up'], 'L0_ffn_gate': _L0_ffn_in['gate'], 'L0_ffn_down': _L0_ffn_in['down'], 'L0_ffn_router': _L0_ffn_in['router'], 'L0_ffn_w_up_s': _L0_ffn_in['w_up_s'], 'L0_ffn_w_gate_s': _L0_ffn_in['w_gate_s'], 'L0_ffn_w_down_s': _L0_ffn_in['w_down_s'], 'L0_c': _L0_c, 'L0_wmod': _L0_wmod, 'L1_attn_Wp': _L1_attn_in['Wp'], 'L1_attn_bp': _L1_attn_in['bp'], 'L1_attn_Wv': _L1_attn_in['Wv'], 'L1_attn_Wo': _L1_attn_in['Wo'], 'L1_ffn_router_w': _L1_ffn_in['router_w'], 'L1_ffn_up_w': _L1_ffn_in['up_w'], 'L1_ffn_gate_w': _L1_ffn_in['gate_w'], 'L1_ffn_down_w': _L1_ffn_in['down_w'], 'L1_ffn_shared_up_w': _L1_ffn_in['shared_up_w'], 'L1_ffn_shared_gate_w': _L1_ffn_in['shared_gate_w'], 'L1_ffn_shared_down_w': _L1_ffn_in['shared_down_w'], 'L1_c': _L1_c, 'L1_wmod': _L1_wmod}
    _x0 = _d['L0_attn_x']
    _d['L0_attn_x'] = jax.random.normal(jax.random.fold_in(jax.random.key(seed), 1), (16, 256, 128), dtype=_x0.dtype)
    del _x0
    return _d

def reference(L0_attn_x, L0_attn_qkv_w, L0_attn_qkv_b, L0_attn_out_w, L0_attn_out_b, L0_attn_g_attn, L0_attn_b_attn, L0_attn_g1, L0_attn_b1, L0_attn_g2, L0_attn_b2, L0_attn_w_ctx, L0_attn_w_x, L0_attn_b_inl, L0_attn_ff_w1, L0_attn_ff_b1, L0_attn_ff_w2, L0_attn_ff_b2, L0_ffn_up, L0_ffn_gate, L0_ffn_down, L0_ffn_router, L0_ffn_w_up_s, L0_ffn_w_gate_s, L0_ffn_w_down_s, L0_c, L0_wmod, L1_attn_Wp, L1_attn_bp, L1_attn_Wv, L1_attn_Wo, L1_ffn_router_w, L1_ffn_up_w, L1_ffn_gate_w, L1_ffn_down_w, L1_ffn_shared_up_w, L1_ffn_shared_gate_w, L1_ffn_shared_down_w, L1_c, L1_wmod):

    def _L0_attn_ref(x, qkv_w, qkv_b, out_w, out_b, g_attn, b_attn, g1, b1, g2, b2, w_ctx, w_x, b_inl, ff_w1, ff_b1, ff_w2, ff_b2):
        import jax, jax.numpy as jnp
        import numpy as np
        B, S, D, H = (2, 256, 128, 16)
        HD = D // H
        FF = 512
        NUM_ITERS = 8
        DT = 0.1
        LN_EPS = 1e-05

        def _ln(x, g, b):
            m = jnp.mean(x, axis=-1, keepdims=True)
            v = jnp.var(x, axis=-1, keepdims=True)
            return (x - m) * jax.lax.rsqrt(v + LN_EPS) * g + b

        def _forward(x, qkv_w, qkv_b, out_w, out_b, g_attn, b_attn, g1, b1, g2, b2, w_ctx, w_x, b_inl, ff_w1, ff_b1, ff_w2, ff_b2):
            b, s, d = x.shape
            xn = _ln(x, g_attn, b_attn)
            qkv = (xn @ qkv_w + qkv_b).reshape(b, s, 3, H, HD)
            qkv = jnp.transpose(qkv, (2, 0, 3, 1, 4))
            q, k, v = (qkv[0], qkv[1], qkv[2])
            scores = jnp.einsum('bhqd,bhkd->bhqk', q, k) / np.sqrt(HD).astype(np.float32)
            causal = jnp.triu(jnp.ones((s, s), dtype=bool), 1)
            scores = jnp.where(causal[None, None], -jnp.inf, scores)
            attn_w = jax.nn.softmax(scores, axis=-1)
            attn = jnp.einsum('bhqk,bhkd->bhqd', attn_w, v)
            attn = jnp.transpose(attn, (0, 2, 1, 3)).reshape(b, s, d)
            attn = attn @ out_w + out_b
            x = x + attn
            ctx = attn.reshape(b * s, d)
            xs = _ln(x, g1, b1).reshape(b * s, d)
            vs = jnp.zeros_like(xs)

            def step(carry, _):
                xs, vs = carry
                u = jnp.tanh(ctx @ w_ctx + xs @ w_x + b_inl)
                vn = vs + DT * (u - xs - vs)
                xn_ = xs + DT * vn
                return ((xn_, vn), None)
            (xs, vs), _ = jax.lax.scan(step, (xs, vs), None, length=NUM_ITERS)
            x = x + xs.reshape(b, s, d)
            h = _ln(x, g2, b2)
            h = jax.nn.gelu(h @ ff_w1 + ff_b1, approximate=False)
            x = x + (h @ ff_w2 + ff_b2)
            return x
        return _forward(x, qkv_w, qkv_b, out_w, out_b, g_attn, b_attn, g1, b1, g2, b2, w_ctx, w_x, b_inl, ff_w1, ff_b1, ff_w2, ff_b2)

    def _L0_ffn_ref(x, up, gate, down, router, w_up_s, w_gate_s, w_down_s):
        import jax, jax.numpy as jnp
        import numpy as np
        B, T, C, H, E = (1, 32, 128, 256, 8)
        STD = 0.02
        b, t, c = x.shape
        x_ = x.reshape(b * t, c)
        logits = x_ @ router.T
        idx = jnp.argmax(logits, axis=-1)
        onehot = jax.nn.one_hot(idx, router.shape[0], dtype=x.dtype)
        u = jnp.einsum('bc,ehc->ebh', x_, up)
        g = jnp.einsum('bc,ehc->ebh', x_, gate)
        h = jax.nn.silu(g) * u
        ye = jnp.einsum('ebh,ech->ebc', h, down)
        y = jnp.einsum('ebc,be->bc', ye, onehot)
        ys = jax.nn.silu(x_ @ w_gate_s.T) * (x_ @ w_up_s.T) @ w_down_s.T
        return (y + ys).reshape(b, t, c)

    def _L1_attn_ref(x, Wp, bp, Wv, Wo):
        import jax, jax.numpy as jnp
        import numpy as np
        B, T, D_MODEL = (2, 128, 128)
        H, DEPTH = (8, 5)
        DH = D_MODEL // H
        Bx, Tx, d = x.shape
        paths = jax.nn.sigmoid(x @ Wp + bp)
        paths = paths.reshape(Bx, Tx, H, DEPTH).transpose(0, 2, 1, 3)
        pq = paths[:, :, :, None, :]
        pk = paths[:, :, None, :, :]
        agree = pq * pk + (1.0 - pq) * (1.0 - pk)
        sim = jnp.cumprod(agree, axis=-1).sum(axis=-1) / DEPTH
        mask = jnp.triu(jnp.ones((Tx, Tx), dtype=bool), k=1)
        sim = jnp.where(mask[None, None], -jnp.inf, sim)
        attn = jax.nn.softmax(sim, axis=-1)
        V = (x @ Wv).reshape(Bx, Tx, H, DH).transpose(0, 2, 1, 3)
        ctx = jnp.einsum('bhqk,bhkd->bhqd', attn, V)
        ctx = ctx.transpose(0, 2, 1, 3).reshape(Bx, Tx, d)
        return ctx @ Wo

    def _L1_ffn_ref(x, router_w, up_w, gate_w, down_w, shared_up_w, shared_gate_w, shared_down_w):
        import jax, jax.numpy as jnp
        import numpy as np
        ALPHA = 2.0
        TOP_K = 2
        logits = jnp.einsum('bsd,de->bse', x, router_w)
        probs = jax.nn.softmax(logits, axis=-1)
        topk_vals, topk_idx = jax.lax.top_k(probs, TOP_K)
        top1_val = topk_vals[..., 0]
        top1_idx = topk_idx[..., 0]
        hid = jnp.einsum('bsd,edh->ebsh', x, up_w) * jax.nn.silu(jnp.einsum('bsd,edh->ebsh', x, gate_w))
        Er = up_w.shape[0]
        mask = (top1_idx[None, :, :] == jnp.arange(Er)[:, None, None]).astype(x.dtype)
        routed = jnp.einsum('ebsh,ehd,ebs->bsd', hid, down_w, mask)
        shid = jnp.einsum('bsd,dh->bsh', x, shared_up_w) * jax.nn.silu(jnp.einsum('bsd,dh->bsh', x, shared_gate_w))
        shared = jnp.einsum('bsh,hd->bsd', shid, shared_down_w)
        return ALPHA * top1_val[..., None] * routed + shared
    x = L0_attn_x
    mod = (_silu(L0_c) @ L0_wmod).reshape(L0_c.shape[0], 6, 1, -1)
    sa, ca, ga, sb, cb, gb = (mod[:, 0], mod[:, 1], mod[:, 2], mod[:, 3], mod[:, 4], mod[:, 5])
    ga = (2 * (ga >= 0) - 1) * jnp.maximum(jnp.abs(ga), 0.25)
    gb = (2 * (gb >= 0) - 1) * jnp.maximum(jnp.abs(gb), 0.25)
    h = _layernorm(x, axis=-1) * (1 + ca) + sa
    x = x + ga * _L0_attn_ref(h, L0_attn_qkv_w, L0_attn_qkv_b, L0_attn_out_w, L0_attn_out_b, L0_attn_g_attn, L0_attn_b_attn, L0_attn_g1, L0_attn_b1, L0_attn_g2, L0_attn_b2, L0_attn_w_ctx, L0_attn_w_x, L0_attn_b_inl, L0_attn_ff_w1, L0_attn_ff_b1, L0_attn_ff_w2, L0_attn_ff_b2)
    h = _layernorm(x, axis=-1) * (1 + cb) + sb
    x = x + gb * _L0_ffn_ref(h, L0_ffn_up, L0_ffn_gate, L0_ffn_down, L0_ffn_router, L0_ffn_w_up_s, L0_ffn_w_gate_s, L0_ffn_w_down_s)
    mod = (_silu(L1_c) @ L1_wmod).reshape(L1_c.shape[0], 6, 1, -1)
    sa, ca, ga, sb, cb, gb = (mod[:, 0], mod[:, 1], mod[:, 2], mod[:, 3], mod[:, 4], mod[:, 5])
    ga = (2 * (ga >= 0) - 1) * jnp.maximum(jnp.abs(ga), 0.25)
    gb = (2 * (gb >= 0) - 1) * jnp.maximum(jnp.abs(gb), 0.25)
    h = _layernorm(x, axis=-1) * (1 + ca) + sa
    x = x + ga * _L1_attn_ref(h, L1_attn_Wp, L1_attn_bp, L1_attn_Wv, L1_attn_Wo)
    h = _layernorm(x, axis=-1) * (1 + cb) + sb
    x = x + gb * _L1_ffn_ref(h, L1_ffn_router_w, L1_ffn_up_w, L1_ffn_gate_w, L1_ffn_down_w, L1_ffn_shared_up_w, L1_ffn_shared_gate_w, L1_ffn_shared_down_w)
    return x

_drawn_inputs = setup_inputs


def setup_inputs(seed=0):
    import zlib

    import numpy as np

    out = dict(_drawn_inputs(seed))
    spreads = {'L0_attn_qkv_b': (0.0, 0.1),
     'L0_attn_out_b': (0.0, 0.1),
     'L0_attn_g_attn': (1.0, 0.6),
     'L0_attn_b_attn': (0.0, 0.1),
     'L0_attn_g1': (1.0, 0.2),
     'L0_attn_b1': (0.0, 0.437),
     'L0_attn_g2': (1.0, 0.6),
     'L0_attn_b2': (0.0, 0.661),
     'L0_attn_b_inl': (0.0, 0.8),
     'L0_attn_ff_b1': (0.0, 0.436),
     'L0_attn_ff_b2': (0.0, 0.405),
     'L1_attn_bp': (0.0, 2.0)}
    factors = {'L0_attn_w_ctx': 6.065,
     'L0_ffn_up': 8.0,
     'L0_ffn_gate': 8.0,
     'L0_ffn_down': 8.0,
     'L0_ffn_router': 8.0,
     'L0_ffn_w_up_s': 8.0,
     'L0_ffn_w_gate_s': 8.0,
     'L0_ffn_w_down_s': 8.0,
     'L1_attn_Wp': 8.0,
     'L1_attn_Wv': 8.0,
     'L1_attn_Wo': 8.0,
     'L1_ffn_router_w': 5.973,
     'L1_ffn_up_w': 5.619,
     'L1_ffn_gate_w': 6.006,
     'L1_ffn_down_w': 5.645,
     'L1_ffn_shared_up_w': 4.182,
     'L1_ffn_shared_gate_w': 4.444,
     'L1_ffn_shared_down_w': 4.174,
     'L1_c': 3.33,
     'L1_wmod': 3.361}
    for name, (base, spread) in spreads.items():
        noise = np.random.default_rng([zlib.crc32(name.encode()), seed]).standard_normal(out[name].shape)
        drawn = base * np.exp(spread * noise) if base else spread * noise
        out[name] = jnp.asarray(drawn.astype(out[name].dtype))
    for name, factor in factors.items():
        out[name] = (out[name] * factor).astype(out[name].dtype)
    return out
```

```python
import concourse.bass as bass
from concourse import mybir
from contextlib import ExitStack

FP32 = mybir.dt.float32
BF16 = mybir.dt.bfloat16
ALU = mybir.AluOpType
ACT = mybir.ActivationFunctionType
AX_X = mybir.AxisListType.X

P = 128
BATCH, SEQ, D = 16, 256, 128
TOK = BATCH * SEQ
CH = 512
NCH = TOK // CH
BPC = CH // SEQ
HEADS0, HD0 = 16, 8
HEADS1, HD1, DEPTH = 8, 16, 5
LEAVES = 2 ** DEPTH
FF = 512
STEPS, DT = 8, 0.1
EPS = 1e-5
E0, HID0 = 8, 256
E1, HID1, R1 = 7, 512, 8
ALPHA = 2.0
SQ = P // 32


def adaln_kernel(nc, a):
    ctx = ExitStack()
    with ctx:
        def sb(name, shape, dt=FP32):
            return ctx.enter_context(nc.sbuf_tensor(name, shape, dt))

        def sem(name):
            return ctx.enter_context(nc.semaphore(name))

        X = sb("X", [P, TOK])
        H = sb("H", [P, TOK])
        N = sb("N", [P, TOK])
        ATT = sb("ATT", [P, TOK])
        XS = sb("XS", [P, TOK])
        V = N
        ident = sb("ident", [P, P])
        identb = sb("identb", [P, P], BF16)
        center = sb("center", [P, P])
        meanm = sb("meanm", [P, P])
        maskqk = sb("maskqk", [P, P], BF16)
        maskkq = sb("maskkq", [P, P], BF16)
        qmask = sb("qmask", [P, 4])
        prefix = sb("prefix", [P, P])
        sel = sb("sel", [8, 8 * P])
        rank = sb("rank", [P, 4 * 8])
        wqkv = sb("wqkv", [P, 3 * D])
        wout = sb("wout", [P, D])
        wctx = sb("wctx", [P, D])
        wx = sb("wx", [P, D])
        wxs = sb("wxs", [P, D])
        w1 = sb("w1", [P, FF])
        w2 = sb("w2", [P, FF // P, D])
        cols = sb("cols", [P, 16])
        b1c = sb("b1c", [P, FF // P])
        vb = sb("vb", [P, 2, D])
        cT = sb("cT", [P, 2, BATCH])
        sc = sb("sc", [P, 2, BATCH])
        wmod = sb("wmod", [P, 2, 6 * D])
        mod = sb("mod", [P, 2, 6, BATCH])
        gsg = sb("gsg", [P, 4, BATCH])
        gab = sb("gab", [P, 4, BATCH])
        wp = sb("wp", [P, HEADS1 * DEPTH])
        bp = sb("bp", [P, 2, HEADS1 * DEPTH])
        wv1 = sb("wv1", [P, D])
        wo1 = sb("wo1", [P, D])
        region = sb("region", [P, 2 * (E0 + 1) * HID0])
        va = region[:, 0:4 * HEADS0 * 64].rearrange("p (a n h c) -> p a n h c", a=2, n=2, c=64)
        va1 = region[:, 0:4 * HEADS1 * 64].rearrange("p (a n h c) -> p a n h c", a=2, n=2, c=64)
        up0 = region[:, 0:(E0 + 1) * HID0].rearrange("p (e h) -> p e h", e=E0 + 1)
        gate0 = region[:, (E0 + 1) * HID0:].rearrange("p (e h) -> p e h", e=E0 + 1)
        down0 = sb("down0", [P, E0 + 1, HID0 // P, D])
        rw0 = sb("rw0", [P, 8])
        up1 = H[:, 0:(E1 + 1) * HID1].rearrange("p (e h) -> p e h", e=E1 + 1)
        gate1 = ATT[:, 0:(E1 + 1) * HID1].rearrange("p (e h) -> p e h", e=E1 + 1)
        down1 = XS[:, 0:(E1 + 1) * HID1].rearrange("p (e j d) -> p e j d", e=E1 + 1, d=D)
        rw1 = sb("rw1", [P, 8])
        sqb = sb("sqb", [P, 4, CH])
        rsb = sb("rsb", [P, 4, CH])
        xnb = sb("xnb", [P, 4, CH])
        nb = sb("nb", [P, 2, SEQ])
        qm = sb("qm", [P, 2, 4, SEQ])
        kf = sb("kf", [P, 2, SEQ])
        mneg = sb("mneg", [P, 2, 4])
        pr = sb("pr", [P, 2, 6 * P])
        pT = sb("pT", [P, 2, 6, P])
        rec = sb("rec", [P, SEQ])
        ao = sb("ao", [P, SEQ])

        lf, lw = qm[:, :, 0:2, :], qm[:, :, 2:4, :]
        zb = sb("zb", [P, 2 * HEADS1 * DEPTH])
        ez = sb("ez", [P, 2 * HEADS1 * DEPTH])
        pq = sb("pq", [P, 2 * HEADS1, DEPTH, 2])
        levels = [None, None] + [sb(f"level{d}", [P, 2 * HEADS1, 2 ** d]) for d in range(2, DEPTH + 1)]
        ncb = xnb[:, 0, :]
        lsb = sb("lsb", [P, 4, 8])
        cand = sb("cand", [P, 4, 8])
        rtop = sb("rtop", [P, 3, 4])
        ohw = sb("ohw", [P, 4, 8])
        ohT = sb("ohT", [8, CH])

        PS = ctx.enter_context(nc.psum_tensor("PS", [P, 8, CH], FP32))

        C_QB, C_KB, C_OUTB, C_GA, C_BA, C_G1, C_B1, C_G2, C_B2, C_INL, C_FB2 = range(11)

        def col(n):
            return cols[:, n:n + 1]

        ld_x, ld_c, ld_a, ld_b, ld_m0, ld_l1, ld_m1 = [sem(f"ld_{n}") for n in ("x", "c", "a", "b", "m0", "l1", "m1")]
        credit = sem("credit")
        mod_silu, mod_ps, mod_done, mod_step = sem("mod_silu"), sem("mod_ps"), sem("mod_done"), sem("mod_step")
        ln_cen, ln_sq, ln_var, ln_lv, ln_rs, ln_xn, ln_out = [sem("ln_" + n) for n in ("cen", "sq", "var", "lv", "rs", "xn", "out")]
        a_nb, a_qkps, a_qsb, a_vps, a_va = [sem("a_" + n) for n in ("nb", "qkps", "qsb", "vps", "va")]
        a_s, a_mx, a_p, a_t, a_ptd, a_pta, a_av = [sem("a_" + n) for n in ("s", "mx", "p", "t", "ptd", "pta", "av")]
        a_ln, a_rec, a_on, a_pj, a_att, a_h = [sem("a_" + n) for n in ("ln", "rec", "on", "pj", "att", "h")]
        i_p, i_u, i_d, i_v, i_x, i_h, i_z, i_w = [sem("i_" + n) for n in ("p", "u", "d", "v", "x", "h", "z", "w")]
        f_h, f_g, f_y, f_hy, f_x = [sem("f_" + n) for n in ("h", "g", "y", "hy", "x")]
        b_nb, b_zv, b_z, b_va, b_ez, b_lv, b_lt, b_lf, b_w, b_lw, b_st = [
            sem("b_" + n) for n in ("nb", "zv", "z", "va", "ez", "lv", "lt", "lf", "w", "lw", "st")]
        b_s, b_p, b_av, b_ln, b_rec, b_on, b_pj, b_x = [
            sem("b_" + n) for n in ("s", "p", "av", "ln", "rec", "on", "pj", "x")]
        m_nc, m_lg, m_st, m_ex, m_oh, m_ohT, m_ohs, m_bc, m_xm, m_u, m_sg, m_hm, m_dn, m_x = [
            sem("m_" + n) for n in ("nc", "lg", "st", "ex", "oh", "ohT", "ohs", "bc", "xm", "u", "sg", "hm", "dn", "x")]
        st_out = sem("st_out")
        va_ones = sem("va_ones")

        block = ctx.enter_context(nc.Block())

        LN_PSC, LN_PSV = 0, 4
        A_PST, A_PSO, A_PSM = 4, 6, 7

        LN_MODA0, LN_ATTN, LN_G1, LN_G2, LN_MODB0, LN_MODA1, LN_MODB1 = range(7)
        LNO = 4

        J0, J1 = (E0 + 1) * (HID0 // P), (E1 + 1) * (HID1 // P)
        MOE = [dict(l=0, E=E0, NH=HID0 // P, up=up0, gate=gate0, down=down0, rw=rw0, J=J0, j0=0, e0=0, ln=LN_MODB0),
               dict(l=1, E=E1, NH=HID1 // P, up=up1, gate=gate1, down=down1, rw=rw1, J=J1, j0=NCH * J0, e0=NCH * E0,
                    ln=LN_MODB1)]

        @block.sync
        def _(sp):
            for dst, src in ((cT, a["cT"]), (wmod, a["wmod"]), (cols, a["cols"]), (center, a["center"]),
                             (meanm, a["meanm"])):
                sp.dma_start(dst[...], src).then_inc(ld_c, 16)
            for t in range(4):
                s = slice(t * TOK // 4, (t + 1) * TOK // 4)
                sp.dma_start(X[:, s], a["xT"][:, s]).then_inc(ld_x, 16)
            for dst, src in ((wqkv, a["wqkv"]), (wout, a["wout"]), (vb, a["vb"]), (qmask, a["qmask"]),
                             (ident, a["ident"]), (identb, a["identb"]), (maskqk, a["maskqk"])):
                sp.dma_start(dst[...], src).then_inc(ld_a, 16)
            for dst, src in ((wctx, a["wctx"]), (wx, a["wx"]), (w1, a["w1"]), (w2, a["w2"]), (b1c, a["b1c"])):
                sp.dma_start(dst[...], src).then_inc(ld_b, 16)
            for dst, src in ((down0, a["down0"]), (rw0, a["rw0"]),
                             (sel, a["sel"]), (rank, a["rank"])):
                sp.dma_start(dst[...], src).then_inc(ld_m0, 16)
            for dst, src in ((wp, a["wp"]), (bp, a["bp"]), (wv1, a["wv1"]), (wo1, a["wo1"]), (prefix, a["prefix"]),
                             (maskkq, a["maskkq"])):
                sp.dma_start(dst[...], src).then_inc(ld_l1, 16)
            sp.dma_start(rw1[:, :], a["rw1"]).then_inc(ld_m1, 16)
            sp.wait_ge(a_av, 8 * BATCH)
            for dst, src in ((up0, a["up0"]), (gate0, a["gate0"])):
                sp.dma_start(dst, src).then_inc(ld_m0, 16)
            sp.wait_ge(i_h, 1)
            for dst, src in ((gate1, a["gate1"]), (down1, a["down1"])):
                sp.dma_start(dst, src).then_inc(ld_m1, 16)
            sp.wait_ge(f_x, NCH)
            sp.dma_start(up1, a["up1"]).then_inc(ld_m1, 16)
            with sp.Fori(0, NCH) as t:
                sp.wait_ge(m_x, NCH + t + 2)
                sp.dma_start(a["out"][:, bass.ds(t * CH, CH)], X[:, bass.ds(t * CH, CH)]).then_inc(st_out, 16)
            sp.wait_ge(st_out, 16 * NCH)

        @block.tensor
        def _(pe):
            def ln(call, src):
                with pe.Fori(0, 2) as i:
                    for pair in range(2):
                        for k in (2 * pair, 2 * pair + 1):
                            t = 8 * call + i * 4 + k
                            pe.wait_ge(ln_xn, t + 1)
                            nc.tensor.matmul(PS[:, LN_PSC + k, :], center[:, :], src[:, bass.ds(i * 4 * CH + k * CH, CH)],
                                             start=True, stop=True).then_inc(ln_cen, 1)
                        for k in (2 * pair, 2 * pair + 1):
                            t = 8 * call + i * 4 + k
                            pe.wait_ge(ln_sq, t + 1)
                            pe.wait_ge(ln_lv, t + 1)
                            nc.tensor.matmul(PS[:, LN_PSV + k % 2, :], meanm[:, :], sqb[:, k, :],
                                             start=True, stop=True).then_inc(ln_var, 1)

            pe.wait_ge(ld_c, 80)
            pe.wait_ge(mod_silu, 1)
            for l in range(2):
                for m in range(6):
                    c = (l * 6 + m) * BATCH
                    last = nc.tensor.matmul(PS[:, 7, c:c + BATCH], wmod[:, l, m * D:(m + 1) * D], sc[:, l, :],
                                            start=True, stop=True)
            last.then_inc(mod_ps, 1)

            pe.wait_ge(ld_x, 64)
            pe.wait_ge(credit, 2)
            ln(LN_MODA0, X)
            pe.wait_ge(ln_out, LNO + 8)
            ln(LN_ATTN, H)
            pe.wait_ge(ln_out, LNO + 16)
            pe.wait_ge(ld_a, 112)

            def scores(b, par, u):
                U = b * 8 + u
                j = u // 2
                r = slice(32 * j, 32 * j + 32)
                s = 2 * (u % 2)
                if u == 0:
                    pe.wait_ge(a_qsb, b + 1)
                for n in range(2):
                    g = 2 * (u % 2) + n
                    nc.tensor.matmul(PS[:, s, n * SEQ:(n + 1) * SEQ], qm[r, par, g, P:SEQ], kf[r, par, :],
                                     start=True, stop=False)
                    nc.tensor.matmul(PS[:, s, n * SEQ + P:(n + 1) * SEQ], identb[:, :], maskqk[:, :],
                                     start=False, stop=True)
                for n in range(2):
                    g = 2 * (u % 2) + n
                    nc.tensor.matmul(PS[:, s + 1, n * P:(n + 1) * P], qm[r, par, g, 0:P], kf[r, par, 0:P],
                                     start=True, stop=False)
                    last = nc.tensor.matmul(PS[:, s + 1, n * P:(n + 1) * P], identb[:, :], maskqk[:, :],
                                            start=False, stop=True)
                last.then_inc(a_s, 1)

            def transposes(U, ub):
                pe.wait_ge(a_p, U + 1)
                if not (type(U) is int and U == 0):
                    pe.wait_ge(a_ptd, U)
                    pe.wait_ge(a_pta, U)
                for n, k in enumerate((4, 0, 5, 2)):
                    nc.tensor.transpose(PS[:, A_PST, n * P:(n + 1) * P], pr[:, ub, k * P:(k + 1) * P], ident[:, :])
                for n, k in enumerate((1, 3)):
                    last = nc.tensor.transpose(PS[:, A_PST + 1, n * P:(n + 1) * P], pr[:, ub, k * P:(k + 1) * P],
                                               ident[:, :])
                last.then_inc(a_t, 1)

            def weigh(U, b, par, u):
                ub = u % 2
                pe.wait_ge(a_ptd, U + 1)
                pe.wait_ge(a_pta, U + 1)
                if u == 0:
                    pe.wait_ge(a_va, b + 1)
                    if not (type(b) is int and b == 0):
                        pe.wait_ge(a_on, b)
                j = u // 2
                half, c = 64 * (j % 2), SEQ * (j // 2)
                for n in range(2):
                    h = 2 * u + n
                    first, end = u % 2 == 0 and n == 0, u % 2 == 1 and n == 1
                    nc.tensor.matmul(PS[half:half + 64, A_PSO, c:c + SEQ], va[:, par, 0, h, :],
                                     pT[:, ub, 2 * n:2 * n + 2, :].rearrange("p n q -> p (n q)"), start=first, stop=False)
                    last = nc.tensor.matmul(PS[half:half + 64, A_PSO, c + P:c + SEQ], va[:, par, 1, h, :],
                                            pT[:, ub, 4 + n, :], start=False, stop=end)
                last.then_inc(a_av, 1)

            def out_project(b):
                pe.wait_ge(a_on, b + 1)
                if not (type(b) is int and b == BATCH - 1):
                    pe.wait_ge(a_va, b + 2)
                nc.tensor.matmul(PS[:, A_PSM, SEQ:2 * SEQ], wout[:, :], ao[:, :], start=True, stop=True).then_inc(a_pj, 1)

            def project_qk(b, par, first=False):
                pe.wait_ge(a_nb, b + 1)
                if not first:
                    pe.wait_ge(a_att, b - 1)
                nc.tensor.matmul(PS[:, A_PSM, 0:SEQ], wqkv[:, 0:D], nb[:, par, :], start=True, stop=True)
                nc.tensor.matmul(PS[:, A_PSM, SEQ:2 * SEQ], wqkv[:, D:2 * D], nb[:, par, :],
                                 start=True, stop=True).then_inc(a_qkps, 1)

            def project_v(b, par):
                pe.wait_ge(a_qsb, b + 1)
                for n in range(2):
                    last = nc.tensor.matmul(PS[:, A_PSM, n * D:(n + 1) * D], nb[:, par, n * P:(n + 1) * P],
                                            wqkv[:, 2 * D:3 * D], start=True, stop=True)
                last.then_inc(a_vps, 1)

            def batch(b, par, head, tail):
                for u in range(8):
                    U = b * 8 + u
                    scores(b, par, u)
                    if u >= 1 or head:
                        transposes(U - 1, (u + 1) % 2)
                    if u >= 2:
                        weigh(U - 2, b, par, u - 2)
                    elif head:
                        weigh(U - 2, b - 1, 1 - par, u + 6)
                    if u == 3 and head:
                        out_project(b - 1)
                    if u == 4 and tail:
                        project_qk(b + 1, 1 - par, first=(type(b) is int and b == 0))
                    if u == 6 and tail:
                        project_v(b + 1, 1 - par)

            project_qk(0, 0, first=True)
            project_v(0, 0)
            batch(0, 0, False, True)
            with pe.Fori(0, BATCH // 2 - 1) as i:
                batch(i * 2 + 1, 1, True, True)
                batch(i * 2 + 2, 0, True, True)
            batch(BATCH - 1, 1, True, False)
            U = 8 * BATCH - 1
            transposes(U, 1)
            weigh(U - 1, BATCH - 1, 1, 6)
            weigh(U, BATCH - 1, 1, 7)
            out_project(BATCH - 1)

            pe.wait_ge(a_h, BATCH)
            ln(LN_G1, H)
            pe.wait_ge(ln_out, LNO + 24)
            pe.wait_ge(ld_b, 80)
            for c in range(NCH):
                s = slice(c * CH, (c + 1) * CH)
                nc.tensor.matmul(PS[:, c, :], wctx[:, :], ATT[:, s], start=True, stop=False)
                nc.tensor.matmul(PS[:, c, :], wx[:, :], XS[:, s], start=False, stop=True).then_inc(i_p, 1)
            pe.wait_ge(i_w, 1)
            with pe.Fori(0, STEPS - 1) as n:
                for c in range(NCH):
                    pe.wait_ge(i_v, n * NCH + c + 5)
                    nc.tensor.matmul(PS[:, c, :], wxs[:, :], V[:, c * CH:(c + 1) * CH], start=False, stop=True,
                                     skip_group_check=True).then_inc(i_p, 1)
            pe.wait_ge(i_h, 1)

            ln(LN_G2, H)
            pe.wait_ge(ln_out, LNO + 32)
            with pe.Fori(0, NCH // 2) as i:
                for k in range(2):
                    t = i * 2 + k
                    for j in range(FF // P):
                        pe.wait_ge(f_g, t * 4 + j + 1)
                        nc.tensor.matmul(PS[:, j, :], w1[:, j * P:(j + 1) * P], N[:, bass.ds(t * CH, CH)],
                                         start=True, stop=True).then_inc(f_h, 1)
                    pe.wait_ge(f_hy, t + 1)
                    for j in range(FF // P):
                        pe.wait_ge(f_g, t * 4 + j + 5)
                        last = nc.tensor.matmul(PS[:, 4 + k, :], w2[:, j, :], sqb[:, j, :],
                                                start=(j == 0), stop=(j == FF // P - 1))
                    last.then_inc(f_y, 1)

            def moe(c):
                E, NH, J, l = c["E"], c["NH"], c["J"], c["l"]
                up, gate, down = c["up"], c["gate"], c["down"]
                with pe.Fori(0, NCH) as t:
                    T = t + NCH * l
                    pe.wait_ge(m_nc, T + 1)
                    pe.wait_ge(m_ohs, T + 1)
                    for n in range(4):
                        last = nc.tensor.matmul(PS[:, 7, n * 8:(n + 1) * 8], ncb[:, n * P:(n + 1) * P], c["rw"][:, :],
                                                start=True, stop=True)
                    last.then_inc(m_lg, 1)

                    def broadcast(e):
                        q = c["e0"] + t * E + e
                        if e == 0:
                            pe.wait_ge(m_oh, T + 1)
                            for n in range(4):
                                last = nc.tensor.transpose(PS[0:8, 7, n * P:(n + 1) * P], ohw[:, n, :], ident[:, :])
                            last.then_inc(m_ohT, 1)
                            pe.wait_ge(m_ohs, T + 2)
                        pe.wait_ge(m_xm, q + 1)
                        nc.tensor.matmul(PS[:, 5 + e % 2, :], sel[:, e * P:(e + 1) * P], ohT[:, :],
                                         start=True, stop=True).then_inc(m_bc, 1)

                    def sum_down(j):
                        pe.wait_ge(m_hm, c["j0"] + t * J + j + 3)
                        e, hb = order[j]
                        m = nc.tensor.matmul(PS[:, 4, :], down[:, e, hb, :], rsb[:, j % 2, :],
                                             start=(j == 0), stop=(j == J - 1))
                        if j == J - 1:
                            m.then_inc(m_dn, 1)

                    order = [(E, hb) for hb in range(NH)] + [(e, hb) for e in range(E) for hb in range(NH)]
                    for j, (e, hb) in enumerate(order):
                        jj = c["j0"] + t * J + j
                        if e < E and hb == 0:
                            pe.wait_ge(m_xm, c["e0"] + t * E + e + 3)
                        pe.wait_ge(m_sg, jj + 1)
                        nc.tensor.matmul(PS[:, j % 2, :], gate[:, e, hb * P:(hb + 1) * P], ncb, start=True, stop=True)
                        pe.wait_ge(m_hm, jj + 1)
                        nc.tensor.matmul(PS[:, 2 + j % 2, :], up[:, e, hb * P:(hb + 1) * P],
                                         ncb if e == E else xnb[:, 1 + e % 2, :], start=True, stop=True).then_inc(m_u, 1)
                        if e == E and hb == NH - 1:
                            broadcast(0)
                        if e < E and hb == 0 and e + 1 < E:
                            broadcast(e + 1)
                        if j:
                            sum_down(j - 1)
                    sum_down(J - 1)

            pe.wait_ge(f_x, NCH)
            ln(LN_MODB0, X)
            pe.wait_ge(ln_out, LNO + 40)
            pe.wait_ge(ld_m0, 96)
            moe(MOE[0])

            pe.wait_ge(m_x, NCH + 1)
            ln(LN_MODA1, X)
            pe.wait_ge(ln_out, LNO + 48)
            pe.wait_ge(ld_l1, 96)

            def project_zv(b, par):
                pe.wait_ge(b_nb, b + 1)
                if not (type(b) is int and b == 0):
                    pe.wait_ge(b_va, b)
                for n in range(2):
                    x = nb[:, par, n * P:(n + 1) * P]
                    nc.tensor.matmul(PS[:, 4, n * 40:(n + 1) * 40], x, wp[:, :], start=True, stop=True)
                    last = nc.tensor.matmul(PS[:, 4, (1 + n) * D:(2 + n) * D], x, wv1[:, :], start=True, stop=True)
                last.then_inc(b_zv, 1)

            def transpose_leaves(b):
                pe.wait_ge(b_lv, b + 1)
                if not (type(b) is int and b == 0):
                    pe.wait_ge(b_lw, b)
                for g in range(2):
                    for n in range(2):
                        h = n * HEADS1 + 4 * g
                        last = nc.tensor.transpose(PS[:, 5, g * SEQ + n * P:g * SEQ + (n + 1) * P],
                                                   levels[DEPTH][:, h:h + 4, :].rearrange("p h l -> p (h l)"), ident[:, :])
                last.then_inc(b_lt, 1)

            def prefix_sums(b, par):
                pe.wait_ge(b_lf, b + 1)
                nc.tensor.matmul(PS[:, 5, :], prefix[:, :], lf[:, par, :, :].rearrange("p g t -> p (g t)"),
                                 start=True, stop=True).then_inc(b_w, 1)

            def scores1(b, par, u):
                r = slice(32 * u, 32 * u + 32)
                s = 2 * (u % 2)
                if u == 0:
                    pe.wait_ge(b_lw, b + 1)
                for n in range(2):
                    o = n * SEQ
                    nc.tensor.matmul(PS[:, s, o:o + SEQ], lw[r, par, n, 0:P], lf[r, par, n, :], start=True, stop=False)
                    nc.tensor.matmul(PS[:, s, o:o + P], identb[:, :], maskkq[:, :], start=False, stop=True)
                for n in range(2):
                    o = n * P
                    nc.tensor.matmul(PS[:, s + 1, o:o + P], lw[r, par, n, P:SEQ], lf[r, par, n, P:SEQ],
                                     start=True, stop=False)
                    last = nc.tensor.matmul(PS[:, s + 1, o:o + P], identb[:, :], maskkq[:, :], start=False, stop=True)
                last.then_inc(b_s, 1)

            def weigh1(U, b, par, u):
                ub = u % 2
                pe.wait_ge(b_p, U + 1)
                if u == 0:
                    pe.wait_ge(b_va, b + 1)
                    if not (type(b) is int and b == 0):
                        pe.wait_ge(b_on, b)
                for n in range(2):
                    h = u + 4 * n
                    j = h // 2
                    half, c = 64 * (j // 2), SEQ * (j % 2)
                    nc.tensor.matmul(PS[half:half + 64, A_PSO, c:c + SEQ], va1[:, par, 0, h, :],
                                     pT[:, ub, 2 * n:2 * n + 2, :].rearrange("p n q -> p (n q)"),
                                     start=(h % 2 == 0), stop=False)
                    last = nc.tensor.matmul(PS[half:half + 64, A_PSO, c + P:c + SEQ], va1[:, par, 1, h, :],
                                            pT[:, ub, 4 + n, :], start=False, stop=(h % 2 == 1))
                last.then_inc(b_av, 1)

            def out_project1(b):
                pe.wait_ge(b_on, b + 1)
                if not (type(b) is int and b == 0):
                    pe.wait_ge(b_x, b)
                nc.tensor.matmul(PS[:, 7, 0:SEQ], wo1[:, :], ao[:, :], start=True, stop=True).then_inc(b_pj, 1)

            def batch1(b, par, head, tail):
                for u in range(4):
                    U = b * 4 + u
                    scores1(b, par, u)
                    if u == 3 and tail:
                        prefix_sums(b + 1, 1 - par)
                    if u:
                        weigh1(U - 1, b, par, u - 1)
                    elif head:
                        weigh1(U - 1, b - 1, 1 - par, 3)
                    if u == 0 and tail:
                        project_zv(b + 1, 1 - par)
                    if u == 2 and head:
                        out_project1(b - 1)
                    if u == 2 and tail:
                        transpose_leaves(b + 1)

            project_zv(0, 0)
            transpose_leaves(0)
            prefix_sums(0, 0)
            batch1(0, 0, False, True)
            with pe.Fori(0, BATCH // 2 - 1) as i:
                batch1(i * 2 + 1, 1, True, True)
                batch1(i * 2 + 2, 0, True, True)
            batch1(BATCH - 1, 1, True, False)
            weigh1(4 * BATCH - 1, BATCH - 1, 1, 3)
            out_project1(BATCH - 1)

            pe.wait_ge(b_x, BATCH)
            ln(LN_MODB1, X)
            pe.wait_ge(ln_out, LNO + 56)
            pe.wait_ge(ld_m1, 64)
            moe(MOE[1])

        @block.scalar
        def _(act):
            nc.scalar.sem_inc(ln_lv, 2)
            nc.scalar.sem_inc(f_g, 4)
            nc.scalar.sem_inc(credit, 1)
            nc.scalar.sem_inc(m_sg, 2)
            act.wait_ge(ld_c, 80)
            nc.scalar.activation(sc[:, :, :], cT[:, :, :], ACT.Silu).then_inc(mod_silu, 1)

            def ln(call):
                with act.Fori(0, 2) as i:
                    for pair in range(2):
                        for k in (2 * pair, 2 * pair + 1):
                            t = 8 * call + i * 4 + k
                            act.wait_ge(ln_cen, t + 1)
                            nc.scalar.activation(sqb[:, k, :], PS[:, LN_PSC + k, :], ACT.Square).then_inc(ln_sq, 1)
                        for k in (2 * pair, 2 * pair + 1):
                            t = 8 * call + i * 4 + k
                            act.wait_ge(ln_var, t + 1)
                            nc.scalar.activation(rsb[:, k, :], PS[:, LN_PSV + k % 2, :], ACT.Ln,
                                                 bias=EPS).then_inc(ln_lv, 1)
                        for k in (2 * pair, 2 * pair + 1):
                            t = 8 * call + i * 4 + k
                            act.wait_ge(ln_lv, t + 3)
                            nc.scalar.activation(rsb[:, k, :], rsb[:, k, :], ACT.Exp, scale=-0.5).then_inc(ln_rs, 1)

            ln(LN_MODA0)
            ln(LN_ATTN)

            act.wait_ge(ld_a, 112)

            def exps(U, u):
                ub, s = u % 2, 2 * (u % 2)
                act.wait_ge(a_mx, U + 1)
                for n in range(2):
                    nc.scalar.activation(pr[:, ub, n * SEQ:(n + 1) * SEQ], PS[:, s, n * SEQ:(n + 1) * SEQ], ACT.Exp,
                                         bias=mneg[:, ub, n:n + 1])
                for n in range(2):
                    last = nc.scalar.activation(pr[:, ub, (4 + n) * P:(5 + n) * P], PS[:, s + 1, n * P:(n + 1) * P],
                                                ACT.Exp, bias=mneg[:, ub, 2 + n:3 + n])
                last.then_inc(a_p, 1)

            def copy_transposed(U, ub):
                act.wait_ge(a_t, U + 1)
                nc.scalar.activation(pT[:, ub, 4:6, :], PS[:, A_PST + 1, 0:2 * P].rearrange("p (n k) -> p n k", n=2),
                                     ACT.Copy).then_inc(a_pta, 1)

            def invert_sums(b):
                act.wait_ge(a_av, 8 * b + 8)
                for j in range(4):
                    half, c = 64 * (j % 2), SEQ * (j // 2)
                    last = nc.scalar.activation(rec[32 * j:32 * j + 32, :], PS[half + 32:half + 64, A_PSO, c:c + SEQ], ACT.Ln)
                last.then_inc(a_ln, 1)
                act.wait_ge(a_ln, b + 1)
                nc.scalar.activation(rec[:, :], rec[:, :], ACT.Exp, scale=-1.0).then_inc(a_rec, 1)

            def add_bias(b):
                act.wait_ge(a_pj, b + 1)
                nc.scalar.activation(ATT[:, bass.ds(b * SEQ, SEQ)], PS[:, A_PSM, SEQ:2 * SEQ], ACT.Identity,
                                     bias=col(C_OUTB)).then_inc(a_att, 1)

            def batch(b, par, head, tail):
                for u in range(8):
                    U = b * 8 + u
                    if u == 2 and head:
                        invert_sums(b - 1)
                    if u >= 1 or head:
                        copy_transposed(U - 1, (u + 1) % 2)
                    exps(U, u)
                    if u == 3 and head:
                        add_bias(b - 1)

            batch(0, 0, False, True)
            with act.Fori(0, BATCH // 2 - 1) as i:
                batch(i * 2 + 1, 1, True, True)
                batch(i * 2 + 2, 0, True, True)
            batch(BATCH - 1, 1, True, False)
            copy_transposed(8 * BATCH - 1, 1)
            invert_sums(BATCH - 1)
            add_bias(BATCH - 1)

            ln(LN_G1)
            with act.Fori(0, STEPS) as n:
                for c in range(NCH):
                    t = n * NCH + c
                    act.wait_ge(i_p, t + 1)
                    act.wait_ge(i_d, t + 1)
                    nc.scalar.activation(sqb[:, c % 4, :], PS[:, c, :], ACT.Tanh, bias=col(C_INL)).then_inc(i_u, 1)

            ln(LN_G2)
            with act.Fori(0, NCH // 2) as i:
                for k in range(2):
                    t = i * 2 + k
                    for j in range(FF // P):
                        act.wait_ge(f_h, t * 4 + j + 1)
                        if j == 0:
                            act.wait_ge(f_y, t + 1)
                        nc.scalar.activation(sqb[:, j, :], PS[:, j, :], ACT.Gelu, bias=b1c[:, j:j + 1]).then_inc(f_g, 1)

            def moe(c):
                J, l = c["J"], c["l"]
                with act.Fori(0, NCH) as t:
                    T = t + NCH * l
                    for j in range(J):
                        jj = c["j0"] + t * J + j
                        if l and j == 0:
                            act.wait_ge(m_st, 4 * NCH + 5 * t + 2)
                            nc.scalar.activation(cand[:, :, :], lsb[:, :, :], ACT.Exp).then_inc(m_ex, 1)
                        act.wait_ge(m_u, jj + 1)
                        act.wait_ge(m_hm, jj + 1)
                        nc.scalar.activation(sqb[:, j % 2, :], PS[:, j % 2, :], ACT.Silu).then_inc(m_sg, 1)

            ln(LN_MODB0)
            moe(MOE[0])
            ln(LN_MODA1)

            def exp_z(b):
                act.wait_ge(b_z, b + 1)
                nc.scalar.activation(ez[:, :], zb[:, :], ACT.Exp, scale=-1.0).then_inc(b_ez, 1)

            def copy_sums(b, par):
                act.wait_ge(b_w, b + 1)
                nc.scalar.activation(lw[:, par, :, :].rearrange("p g t -> p (g t)"), PS[:, 5, :], ACT.Copy).then_inc(b_lw, 1)

            def exps1(U, u):
                ub, s = u % 2, 2 * (u % 2)
                act.wait_ge(b_s, U + 1)
                nc.scalar.activation(pT[:, ub, 0:4, :].rearrange("p n q -> p (n q)"), PS[:, s, :], ACT.Exp, scale=1.0 / DEPTH)
                nc.scalar.activation(pT[:, ub, 4:6, :].rearrange("p n q -> p (n q)"), PS[:, s + 1, 0:SEQ], ACT.Exp,
                                     scale=1.0 / DEPTH).then_inc(b_p, 1)

            def invert_sums1(b):
                act.wait_ge(b_av, 4 * b + 4)
                for j in range(4):
                    half, c = 64 * (j // 2), SEQ * (j % 2)
                    last = nc.scalar.activation(rec[32 * j:32 * j + 32, :], PS[half + 32:half + 64, A_PSO, c:c + SEQ], ACT.Ln)
                last.then_inc(b_ln, 1)
                act.wait_ge(b_ln, b + 1)
                nc.scalar.activation(rec[:, :], rec[:, :], ACT.Exp, scale=-1.0).then_inc(b_rec, 1)

            def batch1(b, par, head, tail):
                for u in range(4):
                    if u == 1 and head:
                        invert_sums1(b - 1)
                    exps1(b * 4 + u, u)
                    if u == 0 and tail:
                        exp_z(b + 1)
                    if u == 3 and tail:
                        copy_sums(b + 1, 1 - par)

            exp_z(0)
            copy_sums(0, 0)
            batch1(0, 0, False, True)
            with act.Fori(0, BATCH // 2 - 1) as i:
                batch1(i * 2 + 1, 1, True, True)
                batch1(i * 2 + 2, 0, True, True)
            batch1(BATCH - 1, 1, True, False)
            invert_sums1(BATCH - 1)

            ln(LN_MODB1)
            moe(MOE[1])

        @block.vector
        def _(dve):
            nc.vector.sem_inc(ln_xn, 4)
            nc.vector.sem_inc(ln_out, LNO)
            nc.vector.sem_inc(i_v, 4)
            nc.vector.sem_inc(f_hy, 2)
            nc.vector.sem_inc(f_y, 1)
            nc.vector.sem_inc(i_x, NCH)
            nc.vector.sem_inc(m_hm, 2)
            nc.vector.sem_inc(m_xm, 2)
            nc.vector.sem_inc(m_x, 1)
            nc.vector.sem_inc(m_ohs, 1)
            nc.vector.sem_inc(credit, 1)

            dve.wait_ge(mod_ps, 1)
            nc.vector.tensor_copy(mod[:, :, :, :].rearrange("p l m b -> p (l m b)"), PS[:, 7, 0:12 * BATCH]).then_inc(mod_step, 1)
            dve.wait_ge(mod_step, 1)
            for l in range(2):
                for n, m in ((0, 2), (1, 5)):
                    nc.vector.tensor_scalar(gsg[:, 2 * l + n, :], mod[:, l, m, :], 0.0, 2.0, ALU.is_ge, ALU.mult)
                    nc.vector.scalar_tensor_tensor(out=gab[:, 2 * l + n, :], in0=mod[:, l, m, :], scalar=-1.0,
                                                   in1=mod[:, l, m, :], op0=ALU.mult, op1=ALU.max)
                for m in (1, 4):
                    last = nc.vector.tensor_scalar(mod[:, l, m, :], mod[:, l, m, :], 1.0, None, ALU.add)
            last.then_inc(mod_step, 1)
            dve.wait_ge(mod_step, 2)
            nc.vector.tensor_scalar(gab[:, :, :], gab[:, :, :], 0.25, None, ALU.max)
            nc.vector.tensor_scalar(gsg[:, :, :], gsg[:, :, :], -1.0, None, ALU.add).then_inc(mod_step, 1)
            dve.wait_ge(mod_step, 3)
            nc.vector.tensor_tensor(gab[:, :, :], gsg[:, :, :], gab[:, :, :], ALU.mult).then_inc(mod_step, 1)
            dve.wait_ge(mod_step, 4)

            def ln(call, dst, scale, shift):
                with dve.Fori(0, 2) as i:
                    for pair in range(2):
                        for k in (2 * pair, 2 * pair + 1):
                            t = 8 * call + i * 4 + k
                            dve.wait_ge(ln_rs, t + 1)
                            dve.wait_ge(ln_out, t + 1)
                            nc.vector.tensor_tensor(xnb[:, k, :], PS[:, LN_PSC + k, :], rsb[:, k, :],
                                                    ALU.mult).then_inc(ln_xn, 1)
                        for k in (2 * pair, 2 * pair + 1):
                            t = 8 * call + i * 4 + k
                            dve.wait_ge(ln_xn, t + 5)
                            if scale.shape[1] == 1:
                                last = nc.vector.tensor_scalar(dst[:, bass.ds(i * 4 * CH + k * CH, CH)], xnb[:, k, :],
                                                               scale, shift, ALU.mult, ALU.add)
                            else:
                                for b in range(BPC):
                                    c = i * 4 * BPC + k * BPC + b
                                    last = nc.vector.tensor_scalar(
                                        dst[:, bass.ds(c * SEQ, SEQ)], xnb[:, k, b * SEQ:(b + 1) * SEQ],
                                        scale[:, bass.ds(c, 1)], shift[:, bass.ds(c, 1)], ALU.mult, ALU.add)
                            last.then_inc(ln_out, 1)

            ln(LN_MODA0, H, mod[:, 0, 1, :], mod[:, 0, 0, :])
            ln(LN_ATTN, N, col(C_GA), col(C_BA))

            dve.wait_ge(ld_a, 112)

            def maxima(U, u):
                ub, s = u % 2, 2 * (u % 2)
                dve.wait_ge(a_s, U + 1)
                nc.vector.reduce_max(mneg[:, ub, 0:2], PS[:, s, :].rearrange("p (n k) -> p n k", n=2), AX_X, negate=True)
                nc.vector.reduce_max(mneg[:, ub, 2:4], PS[:, s + 1, 0:2 * P].rearrange("p (n k) -> p n k", n=2), AX_X,
                                     negate=True).then_inc(a_mx, 1)

            def copy_transposed(U, ub):
                dve.wait_ge(a_t, U + 1)
                nc.vector.tensor_copy(pT[:, ub, 0:4, :].rearrange("p n k -> p (n k)"), PS[:, A_PST, :]).then_inc(a_ptd, 1)

            def queries(b, par):
                dve.wait_ge(a_qkps, b + 1)
                for g in range(4):
                    nc.vector.tensor_scalar(qm[:, par, g, :], PS[:, A_PSM, 0:SEQ], col(C_QB), qmask[:, g:g + 1],
                                                   ALU.add, ALU.mult)
                nc.vector.tensor_scalar(kf[:, par, :], PS[:, A_PSM, SEQ:2 * SEQ], col(C_KB), None, ALU.add).then_inc(a_qsb, 1)

            def values(b, par):
                dve.wait_ge(a_vps, b + 1)
                for g in range(4):
                    last = nc.vector.tensor_tensor(
                        va[:, par, :, g::4, HD0 * g:HD0 * (g + 1)],
                        PS[:, A_PSM, 0:2 * D].rearrange("p (n h d) -> p n h d", n=2, d=HD0)[:, :, g::4, :],
                        vb[:, :, :].rearrange("p n (h d) -> p n h d", d=HD0)[:, :, g::4, :], ALU.add)
                last.then_inc(a_va, 1)

            def normalise(b):
                dve.wait_ge(a_rec, b + 1)
                for j in range(4):
                    half, c = 64 * (j % 2), SEQ * (j // 2)
                    last = nc.vector.tensor_tensor(ao[32 * j:32 * j + 32, :], PS[half:half + 32, A_PSO, c:c + SEQ],
                                                   rec[32 * j:32 * j + 32, :], ALU.mult)
                last.then_inc(a_on, 1)

            def batch(b, par, head, tail):
                for u in range(8):
                    U = b * 8 + u
                    maxima(U, u)
                    if u >= 1 or head:
                        copy_transposed(U - 1, (u + 1) % 2)
                    if u == 2 and head:
                        normalise(b - 1)
                    if u == 4 and tail:
                        queries(b + 1, 1 - par)
                    if u == 6 and tail:
                        values(b + 1, 1 - par)

            queries(0, 0)
            dve.wait_ge(va_ones, 5)
            values(0, 0)
            batch(0, 0, False, True)
            with dve.Fori(0, BATCH // 2 - 1) as i:
                batch(i * 2 + 1, 1, True, True)
                batch(i * 2 + 2, 0, True, True)
            batch(BATCH - 1, 1, True, False)
            copy_transposed(8 * BATCH - 1, 1)
            normalise(BATCH - 1)

            ln(LN_G1, XS, col(C_G1), col(C_B1))
            dve.wait_ge(ld_b, 80)
            nc.vector.tensor_scalar(wxs[:, :], wx[:, :], DT * DT, None, ALU.mult).then_inc(i_w, 1)
            dve.wait_ge(i_z, 1)
            with dve.Fori(0, STEPS) as n:
                def state(c):
                    s = slice(c * CH, (c + 1) * CH)
                    dve.wait_ge(i_v, n * NCH + c + 5)
                    nc.vector.scalar_tensor_tensor(out=XS[:, s], in0=V[:, s], scalar=DT * DT, in1=XS[:, s],
                                                   op0=ALU.mult, op1=ALU.add).then_inc(i_x, 1)
                for c in range(NCH):
                    s = slice(c * CH, (c + 1) * CH)
                    dve.wait_ge(i_d, n * NCH + c + 5)
                    nc.vector.scalar_tensor_tensor(out=V[:, s], in0=V[:, s], scalar=1.0 - DT, in1=rsb[:, c % 4, :],
                                                   op0=ALU.mult, op1=ALU.add).then_inc(i_v, 1)
                    if c:
                        state(c - 1)
                state(NCH - 1)

            dve.wait_ge(i_h, 1)
            ln(LN_G2, N, col(C_G2), col(C_B2))
            with dve.Fori(0, NCH // 2) as i:
                for k in range(2):
                    t = i * 2 + k
                    dve.wait_ge(f_y, t + 2)
                    nc.vector.scalar_tensor_tensor(out=H[:, bass.ds(t * CH, CH)], in0=PS[:, 4 + k, :], scalar=col(C_FB2),
                                                   in1=H[:, bass.ds(t * CH, CH)], op0=ALU.add, op1=ALU.add).then_inc(f_hy, 1)
                    dve.wait_ge(f_hy, t + 3)
                    for b in range(BPC):
                        c = t * BPC + b
                        last = nc.vector.scalar_tensor_tensor(
                            out=X[:, bass.ds(c * SEQ, SEQ)], in0=H[:, bass.ds(c * SEQ, SEQ)], scalar=gab[:, 0, bass.ds(c, 1)],
                            in1=X[:, bass.ds(c * SEQ, SEQ)], op0=ALU.mult, op1=ALU.add)
                    last.then_inc(f_x, 1)

            def moe(c):
                E, J, l = c["E"], c["J"], c["l"]
                with dve.Fori(0, NCH) as t:
                    T = t + NCH * l

                    def item(j):
                        jj = c["j0"] + t * J + j
                        dve.wait_ge(m_sg, jj + 3)
                        nc.vector.tensor_tensor(rsb[:, j % 2, :], sqb[:, j % 2, :], PS[:, 2 + j % 2, :],
                                                ALU.mult).then_inc(m_hm, 1)

                    def masked(e):
                        dve.wait_ge(m_bc, c["e0"] + t * E + e + 1)
                        nc.vector.tensor_tensor(xnb[:, 1 + e % 2, :], ncb, PS[:, 5 + e % 2, :], ALU.mult).then_inc(m_xm, 1)

                    S = 4 * t if l == 0 else 4 * NCH + 5 * t
                    dve.wait_ge(m_lg, T + 1)
                    lg = PS[:, 7, 0:32].rearrange("p (n e) -> p n e", n=4)

                    def wide(x):
                        return x.rearrange("p (n o) -> p n o", o=1).to_broadcast([P, 4, 8])

                    nc.vector.reduce_max(rtop[:, 0, :], lg, AX_X).then_inc(m_st, 1)
                    dve.wait_ge(m_st, S + 1)
                    nc.vector.tensor_tensor(lsb[:, :, :], lg, wide(rtop[:, 0, :]), ALU.subtract).then_inc(m_st, 1)
                    dve.wait_ge(m_st, S + 2)
                    if l:
                        dve.wait_ge(m_ex, t + 1)
                        nc.vector.reduce_sum(rtop[:, 1, :], cand[:, :, :], AX_X)
                    nc.vector.scalar_tensor_tensor(out=ohw[:, :, :], in0=lsb[:, :, :], scalar=0.0,
                                                   in1=rank[:, :].rearrange("p (n e) -> p n e", n=4),
                                                   op0=ALU.is_equal, op1=ALU.mult).then_inc(m_st, 1)
                    dve.wait_ge(m_st, S + 3)
                    last = nc.vector.reduce_max(rtop[:, 0, :], ohw[:, :, :], AX_X)
                    if l:
                        last = nc.vector.reciprocal(rtop[:, 2, :], rtop[:, 1, :])
                    last.then_inc(m_st, 1)
                    dve.wait_ge(m_st, S + 4)
                    nc.vector.tensor_tensor(ohw[:, :, :], ohw[:, :, :], wide(rtop[:, 0, :]),
                                            ALU.is_equal).then_inc(m_st if l else m_oh, 1)
                    if l:
                        dve.wait_ge(m_st, S + 5)
                        nc.vector.scalar_tensor_tensor(out=ohw[:, :, :], in0=ohw[:, :, :], scalar=ALPHA,
                                                       in1=wide(rtop[:, 2, :]), op0=ALU.mult, op1=ALU.mult).then_inc(m_oh, 1)
                    NH = c["NH"]
                    for j in range(NH - 1):
                        item(j)
                    dve.wait_ge(m_ohT, T + 1)
                    nc.vector.tensor_copy(ohT[:, :], PS[0:8, 7, :]).then_inc(m_ohs, 1)
                    masked(0)
                    item(NH - 1)
                    for e in range(E):
                        for hb in range(NH):
                            item(NH + e * NH + hb)
                            if hb == 0 and e + 1 < E:
                                masked(e + 1)
                    dve.wait_ge(m_dn, T + 1)
                    for b in range(BPC):
                        q = t * BPC + b
                        last = nc.vector.scalar_tensor_tensor(
                            out=X[:, bass.ds(q * SEQ, SEQ)], in0=PS[:, 4, b * SEQ:(b + 1) * SEQ],
                            scalar=gab[:, 2 * l + 1, bass.ds(q, 1)], in1=X[:, bass.ds(q * SEQ, SEQ)],
                            op0=ALU.mult, op1=ALU.add)
                    last.then_inc(m_x, 1)

            ln(LN_MODB0, N, mod[:, 0, 4, :], mod[:, 0, 3, :])
            dve.wait_ge(ld_m0, 96)
            moe(MOE[0])
            dve.wait_ge(m_x, NCH + 1)
            ln(LN_MODA1, N, mod[:, 1, 1, :], mod[:, 1, 0, :])

            dve.wait_ge(ld_l1, 96)

            def values1(b, par):
                dve.wait_ge(b_zv, b + 1)
                nc.vector.tensor_tensor(zb[:, :], PS[:, 4, 0:80], bp[:, :, :].rearrange("p n z -> p (n z)"), ALU.add).then_inc(b_z, 1)
                for g in range(2):
                    last = nc.vector.tensor_copy(
                        va1[:, par, :, g::2, HD1 * g:HD1 * (g + 1)],
                        PS[:, 4, D:3 * D].rearrange("p (n h d) -> p n h d", n=2, d=HD1)[:, :, g::2, :])
                last.then_inc(b_va, 1)

            def leaves(b):
                dve.wait_ge(b_ez, b + 1)
                L = b * 6
                nc.vector.tensor_scalar(ez[:, :], ez[:, :], 1.0, None, ALU.add).then_inc(b_st, 1)
                dve.wait_ge(b_st, L + 1)
                e = ez[:, :].rearrange("p (h d o) -> p h d o", d=DEPTH, o=1)
                nc.vector.reciprocal(pq[:, :, :, 0:1], e).then_inc(b_st, 1)
                dve.wait_ge(b_st, L + 2)
                nc.vector.tensor_scalar(pq[:, :, :, 1:2], pq[:, :, :, 0:1], -1.0, 1.0, ALU.mult, ALU.add).then_inc(b_st, 1)
                for d in range(2, DEPTH + 1):
                    dve.wait_ge(b_st, L + d + 1)
                    m = 2 ** (d - 1)
                    up = (pq[:, :, 0, :] if d == 2 else levels[d - 1][:, :, :]).rearrange("p h (m o) -> p h m o", o=1)
                    step = pq[:, :, d - 1:d, :]
                    last = nc.vector.tensor_tensor(levels[d][:, :, :].rearrange("p h (m o) -> p h m o", o=2),
                                                   up.to_broadcast([P, 2 * HEADS1, m, 2]),
                                                   step.to_broadcast([P, 2 * HEADS1, m, 2]), ALU.mult)
                    last.then_inc(b_lv if d == DEPTH else b_st, 1)

            def copy_leaves(b, par):
                dve.wait_ge(b_lt, b + 1)
                nc.vector.tensor_copy(lf[:, par, :, :].rearrange("p g t -> p (g t)"), PS[:, 5, :]).then_inc(b_lf, 1)

            def normalise1(b):
                dve.wait_ge(b_rec, b + 1)
                for j in range(4):
                    half, c = 64 * (j // 2), SEQ * (j % 2)
                    last = nc.vector.tensor_tensor(ao[32 * j:32 * j + 32, :], PS[half:half + 32, A_PSO, c:c + SEQ],
                                                   rec[32 * j:32 * j + 32, :], ALU.mult)
                last.then_inc(b_on, 1)

            def residual1(b):
                dve.wait_ge(b_pj, b + 1)
                s = bass.ds(b * SEQ, SEQ)
                nc.vector.scalar_tensor_tensor(out=X[:, s], in0=PS[:, 7, 0:SEQ], scalar=gab[:, 2, bass.ds(b, 1)],
                                               in1=X[:, s], op0=ALU.mult, op1=ALU.add).then_inc(b_x, 1)

            def batch1(b, par, head, tail):
                if tail:
                    values1(b + 1, 1 - par)
                if head:
                    normalise1(b - 1)
                if tail:
                    leaves(b + 1)
                if head:
                    residual1(b - 1)
                if tail:
                    copy_leaves(b + 1, 1 - par)

            dve.wait_ge(va_ones, 8)
            values1(0, 0)
            leaves(0)
            copy_leaves(0, 0)
            batch1(0, 0, False, True)
            with dve.Fori(0, BATCH // 2 - 1) as i:
                batch1(i * 2 + 1, 1, True, True)
                batch1(i * 2 + 2, 0, True, True)
            batch1(BATCH - 1, 1, True, False)
            normalise1(BATCH - 1)
            residual1(BATCH - 1)

            dve.wait_ge(b_x, BATCH)
            ln(LN_MODB1, N, mod[:, 1, 4, :], mod[:, 1, 3, :])
            moe(MOE[1])

        @block.gpsimd
        def _(pool):
            nc.gpsimd.sem_inc(i_d, 4)

            def stage(b, par):
                if not (type(b) is int and b < 2):
                    pool.wait_ge(a_vps, b - 1)
                nc.gpsimd.tensor_copy(nb[:, par, :], N[:, bass.ds(b * SEQ, SEQ)]).then_inc(a_nb, 1)

            def residual(b):
                pool.wait_ge(a_att, b + 1)
                s = bass.ds(b * SEQ, SEQ)
                nc.gpsimd.tensor_tensor(H[:, s], H[:, s], ATT[:, s], ALU.add).then_inc(a_h, 1)

            def clear_values(x, count, width):
                nc.gpsimd.memset(x, 0.0).then_inc(va_ones, 1)
                for g in range(32 // width):
                    pool.wait_ge(va_ones, count + 1)
                    nc.gpsimd.memset(x[:, :, :, g::32 // width, 32 + width * g:32 + width * (g + 1)], 1.0).then_inc(va_ones, 1)

            clear_values(va, 0, HD0)
            pool.wait_ge(ln_out, LNO + 16)
            stage(0, 0)
            stage(1, 1)
            with pool.Fori(0, BATCH // 2 - 1) as i:
                for k in range(2):
                    stage(i * 2 + k + 2, k)
                    residual(i * 2 + k)
            residual(BATCH - 2)
            residual(BATCH - 1)

            pool.wait_ge(a_vps, BATCH)
            nc.gpsimd.memset(V[:, :], 0.0).then_inc(i_z, 1)
            pool.wait_ge(ln_out, LNO + 24)
            with pool.Fori(0, STEPS) as n:
                for c in range(NCH):
                    t = n * NCH + c
                    pool.wait_ge(i_u, t + 1)
                    pool.wait_ge(i_x, t + 1)
                    pool.wait_ge(i_v, t + 1)
                    nc.gpsimd.tensor_tensor(rsb[:, c % 4, :], sqb[:, c % 4, :], XS[:, c * CH:(c + 1) * CH],
                                            ALU.subtract).then_inc(i_d, 1)
            pool.wait_ge(i_x, NCH + STEPS * NCH)
            nc.gpsimd.tensor_tensor(H[:, :], H[:, :], XS[:, :], ALU.add).then_inc(i_h, 1)

            def moe(c):
                J, l = c["J"], c["l"]
                pool.wait_ge(ln_out, LNO + 8 * c["ln"] + 8)
                with pool.Fori(0, NCH) as t:
                    pool.wait_ge(m_x, t + NCH * l + 1)
                    nc.gpsimd.tensor_copy(ncb, N[:, bass.ds(t * CH, CH)]).then_inc(m_nc, 1)

            moe(MOE[0])

            def stage1(b, par):
                if not (type(b) is int and b < 2):
                    pool.wait_ge(b_zv, b - 1)
                nc.gpsimd.tensor_copy(nb[:, par, :], N[:, bass.ds(b * SEQ, SEQ)]).then_inc(b_nb, 1)

            pool.wait_ge(m_x, NCH + 1)
            clear_values(va1, 5, HD1)
            pool.wait_ge(ln_out, LNO + 48)
            stage1(0, 0)
            stage1(1, 1)
            with pool.Fori(0, BATCH // 2 - 1) as i:
                for k in range(2):
                    stage1(i * 2 + k + 2, k)
            moe(MOE[1])


def kernel(**inputs):
    import numpy as np
    import ml_dtypes
    import concourse.bacc as _bacc
    from concourse.bass_utils import run_bass_kernel_spmd as _run

    g = {k: np.asarray(v) for k, v in inputs.items()}
    f = np.float32
    nc = _bacc.Bacc("TRN2", target_bir_lowering=False, num_devices=1)
    arr = {}
    arr["xT"] = g["L0_attn_x"].reshape(TOK, D).T
    arr["cT"] = np.stack([g["L0_c"].T, g["L1_c"].T], 1)
    arr["wmod"] = np.stack([g["L0_wmod"], g["L1_wmod"]], 1)
    names = ["L0_attn_out_b", "L0_attn_g_attn", "L0_attn_b_attn", "L0_attn_g1", "L0_attn_b1", "L0_attn_g2",
             "L0_attn_b2", "L0_attn_b_inl", "L0_attn_ff_b2"]
    qb = g["L0_attn_qkv_b"].reshape(3, D)
    arr["cols"] = np.stack([qb[0], qb[1]] + [g[n] for n in names] + [np.zeros(D, f)] * 5, 1)
    arr["center"] = (np.eye(D) - 1.0 / D).astype(f)
    arr["meanm"] = np.full((D, D), 1.0 / D, f)
    arr["ident"] = np.eye(P, dtype=f)
    arr["identb"] = np.eye(P).astype(ml_dtypes.bfloat16)
    q, k = np.arange(P)[:, None], np.arange(P)[None, :]
    arr["maskqk"] = np.where(k > q, -1e30, 0.0).astype(ml_dtypes.bfloat16)
    arr["maskkq"] = np.where(k < q, -1e30, 0.0).astype(ml_dtypes.bfloat16)
    arr["qmask"] = np.where((np.arange(P)[:, None] % 32) // HD0 == np.arange(4)[None, :], HD0 ** -0.5, 0.0).astype(f)
    arr["vb"] = np.broadcast_to(qb[2], (P, 2, D))
    arr["wqkv"] = g["L0_attn_qkv_w"]
    arr["wout"] = g["L0_attn_out_w"]
    arr["wctx"] = g["L0_attn_w_ctx"]
    arr["wx"] = g["L0_attn_w_x"]
    arr["w1"] = g["L0_attn_ff_w1"]
    arr["w2"] = g["L0_attn_ff_w2"].reshape(FF // P, P, D).transpose(1, 0, 2)
    arr["b1c"] = g["L0_attn_ff_b1"].reshape(FF // P, P).T
    up = np.concatenate([g["L0_ffn_up"], g["L0_ffn_w_up_s"][None]], 0)
    gate = np.concatenate([g["L0_ffn_gate"], g["L0_ffn_w_gate_s"][None]], 0)
    down = np.concatenate([g["L0_ffn_down"], g["L0_ffn_w_down_s"][None]], 0)
    arr["up0"] = up.transpose(2, 0, 1)
    arr["gate0"] = gate.transpose(2, 0, 1)
    arr["down0"] = down.reshape(E0 + 1, D, HID0 // P, P).transpose(3, 0, 2, 1)
    arr["rw0"] = g["L0_ffn_router"].T
    up = np.concatenate([g["L1_ffn_up_w"], g["L1_ffn_shared_up_w"][None]], 0)
    gate = np.concatenate([g["L1_ffn_gate_w"], g["L1_ffn_shared_gate_w"][None]], 0)
    down = np.concatenate([g["L1_ffn_down_w"], g["L1_ffn_shared_down_w"][None]], 0)
    arr["up1"] = up.transpose(1, 0, 2)
    arr["gate1"] = gate.transpose(1, 0, 2)
    arr["down1"] = down.reshape(E1 + 1, HID1 // P, P, D).transpose(2, 0, 1, 3)
    arr["rw1"] = g["L1_ffn_router_w"]
    arr["wp"] = g["L1_attn_Wp"]
    arr["bp"] = np.broadcast_to(g["L1_attn_bp"], (P, 2, HEADS1 * DEPTH))
    arr["wv1"] = g["L1_attn_Wv"]
    arr["wo1"] = g["L1_attn_Wo"]
    x = np.arange(LEAVES)[:, None] ^ np.arange(LEAVES)[None, :]
    arr["prefix"] = np.kron(np.eye(SQ), np.sum([x < 2 ** n for n in range(DEPTH)], 0)).astype(f)
    arr["sel"] = np.kron(np.eye(8), np.ones((1, P))).astype(f)
    arr["rank"] = np.broadcast_to(np.tile(8.0 - np.arange(8), 4), (P, 32)).astype(f)
    arrays, args = {}, {}
    for n, v in arr.items():
        v = np.ascontiguousarray(v)
        arrays[n + "_dram"] = v
        args[n] = nc.dram_tensor(n + "_dram", v.shape, mybir.dt.from_np(v.dtype), kind="ExternalInput").ap()
    args["out"] = nc.dram_tensor("out_dram", (D, TOK), FP32, kind="ExternalOutput").ap()
    adaln_kernel(nc, args)
    r = _run(nc, [arrays], core_ids=[0])
    return np.ascontiguousarray(r.results[0]["out_dram"].T).reshape(BATCH, SEQ, D)
```

```python
import concourse.bass as bass
from concourse import mybir
from contextlib import ExitStack

FP32 = mybir.dt.float32
BF16 = mybir.dt.bfloat16
ALU = mybir.AluOpType
ACT = mybir.ActivationFunctionType
AX_X = mybir.AxisListType.X

P = 128
BATCH, SEQ, D = 16, 256, 128
TOK = BATCH * SEQ
CH = 512
NCH = TOK // CH
BPC = CH // SEQ
HEADS0, HD0 = 16, 8
HEADS1, HD1, DEPTH = 8, 16, 5
LEAVES = 2 ** DEPTH
FF = 512
STEPS, DT = 8, 0.1
EPS = 1e-5
E0, HID0 = 8, 256
E1, HID1, R1 = 7, 512, 8
ALPHA = 2.0
TILES = TOK // P
SLOTS = TILES + 7
ROW = D + 2
RING = 6
SQ = P // 32


def adaln_kernel(nc, a):
    ctx = ExitStack()
    with ctx:
        def sb(name, shape, dt=FP32):
            return ctx.enter_context(nc.sbuf_tensor(name, shape, dt))

        def sem(name):
            return ctx.enter_context(nc.semaphore(name))

        X = sb("X", [P, TOK])
        H = sb("H", [P, TILES * ROW])
        N = sb("N", [P, TOK])
        ATT = sb("ATT", [P, TOK])
        XS = sb("XS", [P, TOK])
        V = N
        ident = sb("ident", [P, P])
        identb = sb("identb", [P, P], BF16)
        center = sb("center", [P, P])
        meanm = sb("meanm", [P, P])
        maskqk = sb("maskqk", [P, P], BF16)
        maskkq = sb("maskkq", [P, P], BF16)
        qmask = sb("qmask", [P, 4])
        prefix = sb("prefix", [P, P])
        before = sb("before", [P, P])
        ones = sb("ones", [P, P])
        rank = sb("rank", [P, 8])
        upto = sb("upto", [P, 8, 8])
        tile_starts = sb("tile_starts", [P, 40])
        tile_ids = sb("tile_ids", [P, 40])
        token_ids = sb("token_ids", [P, TILES], mybir.dt.int32)
        wqkv = sb("wqkv", [P, 3 * D])
        wout = sb("wout", [P, D])
        wctx = sb("wctx", [P, D])
        wx = sb("wx", [P, D])
        wxs = sb("wxs", [P, D])
        w1 = sb("w1", [P, FF])
        w2 = sb("w2", [P, FF // P, D])
        cols = sb("cols", [P, 16])
        b1c = sb("b1c", [P, FF // P])
        vb = sb("vb", [P, 2, D])
        cT = sb("cT", [P, 2, BATCH])
        sc = sb("sc", [P, 2, BATCH])
        wmod = sb("wmod", [P, 2, 6 * D])
        mod = sb("mod", [P, 2, 6, BATCH])
        gsg = sb("gsg", [P, 4, BATCH])
        gab = sb("gab", [P, 4, BATCH])
        wp = sb("wp", [P, HEADS1 * DEPTH])
        bp = sb("bp", [P, 2, HEADS1 * DEPTH])
        wv1 = sb("wv1", [P, D])
        wo1 = sb("wo1", [P, D])
        region = sb("region", [P, 2 * (E0 + 1) * HID0])
        va = region[:, 0:4 * HEADS0 * 64].rearrange("p (a n h c) -> p a n h c", a=2, n=2, c=64)
        va1 = region[:, 0:4 * HEADS1 * 64].rearrange("p (a n h c) -> p a n h c", a=2, n=2, c=64)
        up0 = region[:, 0:(E0 + 1) * HID0].rearrange("p (e h) -> p e h", e=E0 + 1)
        gate0 = region[:, (E0 + 1) * HID0:].rearrange("p (e h) -> p e h", e=E0 + 1)
        down0 = sb("down0", [P, E0 + 1, HID0 // P, D])
        rw0 = sb("rw0", [P, 8])
        up1 = H[:, 0:(E1 + 1) * HID1].rearrange("p (e h) -> p e h", e=E1 + 1)
        gate1 = ATT[:, 0:(E1 + 1) * HID1].rearrange("p (e h) -> p e h", e=E1 + 1)
        down1 = XS[:, 0:(E1 + 1) * HID1].rearrange("p (e j d) -> p e j d", e=E1 + 1, d=D)
        rw1 = sb("rw1", [P, 8])
        sqb = sb("sqb", [P, 4, CH])
        rsb = sb("rsb", [P, 4, CH])
        xnb = sb("xnb", [P, 4, CH])
        nb = sb("nb", [P, 2, SEQ])
        qm = sb("qm", [P, 2, 4, SEQ])
        kf = sb("kf", [P, 2, SEQ])
        mneg = sb("mneg", [P, 2, 4])
        pr = sb("pr", [P, 2, 6 * P])
        pT = sb("pT", [P, 2, 6, P])
        rec = sb("rec", [P, SEQ])
        ao = sb("ao", [P, SEQ])

        lf, lw = qm[:, :, 0:2, :], qm[:, :, 2:4, :]
        zb = sb("zb", [P, 2 * HEADS1 * DEPTH])
        ez = sb("ez", [P, 2 * HEADS1 * DEPTH])
        pq = sb("pq", [P, 2 * HEADS1, DEPTH, 2])
        levels = [None, None] + [sb(f"level{d}", [P, 2 * HEADS1, 2 ** d]) for d in range(2, DEPTH + 1)]
        def table(x, n):
            return x[:, n * 256:(n + 1) * 256].rearrange("p (t e) -> p t e", e=8)

        qm_flat = qm[:, :, :, :].rearrange("p a g t -> p (a g t)")
        pr_flat = pr[:, :, :].rearrange("p a t -> p (a t)")
        lgt, less, expl, cand, onehot, cnt_a, cnt_b = [table(qm_flat, n) for n in range(7)]
        steps8 = pr_flat[:, 0:320]
        place = table(pr_flat, 2)
        small = sb("small", [P, 8, 40])
        pos = sb("pos", [P, TILES], mybir.dt.int32)
        eid = sb("eid", [P, 40], mybir.dt.int32)
        slot_in = sb("slot_in", [P, RING, ROW])
        slot_out = xnb[:, 2:4, :].rearrange("p a (b d) -> p (a b) d", d=D)
        rows = [H[:, :].rearrange("p (t c) -> p t c", c=ROW), region[:, 0:TILES * ROW].rearrange("p (t c) -> p t c", c=ROW)]
        sorted_rows = [nc.dram_tensor(f"sorted_rows{l}", (SLOTS * P, ROW), FP32) for l in range(2)]
        token_rows = [nc.dram_tensor(f"token_rows{l}", (TOK + SLOTS * P, D), FP32) for l in range(2)]

        PS = ctx.enter_context(nc.psum_tensor("PS", [P, 8, CH], FP32))

        C_QB, C_KB, C_OUTB, C_GA, C_BA, C_G1, C_B1, C_G2, C_B2, C_INL, C_FB2 = range(11)

        def col(n):
            return cols[:, n:n + 1]

        ld_x, ld_c, ld_a, ld_b, ld_m0, ld_l1, ld_m1 = [sem(f"ld_{n}") for n in ("x", "c", "a", "b", "m0", "l1", "m1")]
        credit = sem("credit")
        mod_silu, mod_ps, mod_done, mod_step = sem("mod_silu"), sem("mod_ps"), sem("mod_done"), sem("mod_step")
        ln_cen, ln_sq, ln_var, ln_lv, ln_rs, ln_xn, ln_out = [sem("ln_" + n) for n in ("cen", "sq", "var", "lv", "rs", "xn", "out")]
        a_nb, a_qkps, a_qsb, a_vps, a_va = [sem("a_" + n) for n in ("nb", "qkps", "qsb", "vps", "va")]
        a_s, a_mx, a_p, a_t, a_ptd, a_pta, a_av = [sem("a_" + n) for n in ("s", "mx", "p", "t", "ptd", "pta", "av")]
        a_ln, a_rec, a_on, a_pj, a_att, a_h = [sem("a_" + n) for n in ("ln", "rec", "on", "pj", "att", "h")]
        i_p, i_u, i_d, i_v, i_x, i_h, i_z, i_w = [sem("i_" + n) for n in ("p", "u", "d", "v", "x", "h", "z", "w")]
        f_h, f_g, f_y, f_hy, f_x = [sem("f_" + n) for n in ("h", "g", "y", "hy", "x")]
        b_nb, b_zv, b_z, b_va, b_ez, b_lv, b_lt, b_lf, b_w, b_lw, b_st = [
            sem("b_" + n) for n in ("nb", "zv", "z", "va", "ez", "lv", "logits", "lf", "w", "lw", "st")]
        b_s, b_p, b_av, b_ln, b_rec, b_on, b_pj, b_x = [
            sem("b_" + n) for n in ("s", "p", "av", "ln", "rec", "on", "pj", "x")]
        RS = [{n: sem(f"r{l}_{n}") for n in (
            "staged", "xt", "xt_sb", "logits", "logits_sb", "exp", "onehot", "counts", "step", "pos",
            "fill", "dispatched", "s_up", "s_silu", "s_hidden", "s_sum", "s_x",
            "xk", "xf", "up", "silu", "hidden", "ht", "hf", "down", "y", "back", "x")} for l in range(2)]
        for l in range(2):
            RS[l]["load"] = [sem(f"r{l}_load{n}") for n in range(RING)]
            RS[l]["sent"] = [sem(f"r{l}_sent{n}") for n in range(RING)]
            RS[l]["rows"] = [sem(f"r{l}_rows{n}") for n in range(2)]
        st_out = sem("st_out")
        va_ones = sem("va_ones")

        block = ctx.enter_context(nc.Block())

        LN_PSC, LN_PSV = 0, 4
        A_PST, A_PSO, A_PSM = 4, 6, 7
        B_PSO = 6

        LN_EXP = "natural_log_exp_and_others"
        LN_MODA0, LN_ATTN, LN_G1, LN_G2, LN_MODB0, LN_MODA1, LN_MODB1 = range(7)
        LNO = 4

        LD_M0 = 11 * 16
        MOE = [dict(l=0, E=E0, NH=HID0 // P, HID=HID0, up=up0, gate=gate0, down=down0, rw=rw0, cap=E0 - 1, ln=LN_MODB0),
               dict(l=1, E=E1, NH=HID1 // P, HID=HID1, up=up1, gate=gate1, down=down1, rw=rw1, cap=E1 - 1, ln=LN_MODB1)]
        LOOPED = (SLOTS - 3) // RING - 1
        LOADS = [(SLOTS - r + RING - 1) // RING for r in range(RING)]

        @block.sync
        def _(sp):
            for dst, src in ((cT, a["cT"]), (wmod, a["wmod"]), (cols, a["cols"]), (center, a["center"]),
                             (meanm, a["meanm"])):
                sp.dma_start(dst[...], src).then_inc(ld_c, 16)
            for t in range(4):
                s = slice(t * TOK // 4, (t + 1) * TOK // 4)
                sp.dma_start(X[:, s], a["xT"][:, s]).then_inc(ld_x, 16)
            for dst, src in ((wqkv, a["wqkv"]), (wout, a["wout"]), (vb, a["vb"]), (qmask, a["qmask"]),
                             (ident, a["ident"]), (identb, a["identb"]), (maskqk, a["maskqk"])):
                sp.dma_start(dst[...], src).then_inc(ld_a, 16)
            for dst, src in ((wctx, a["wctx"]), (wx, a["wx"]), (w1, a["w1"]), (w2, a["w2"]), (b1c, a["b1c"])):
                sp.dma_start(dst[...], src).then_inc(ld_b, 16)
            for dst, src in ((down0, a["down0"]), (rw0, a["rw0"]),
                             (rank, a["rank"]), (before, a["before"]), (ones, a["ones"]), (upto, a["upto"]),
                             (tile_starts, a["tile_starts"]), (tile_ids, a["tile_ids"]), (token_ids, a["token_ids"])):
                sp.dma_start(dst[...], src).then_inc(ld_m0, 16)
            for dst, src in ((wp, a["wp"]), (bp, a["bp"]), (wv1, a["wv1"]), (wo1, a["wo1"]), (prefix, a["prefix"]),
                             (maskkq, a["maskkq"])):
                sp.dma_start(dst[...], src).then_inc(ld_l1, 16)
            sp.dma_start(rw1[:, :], a["rw1"]).then_inc(ld_m1, 16)
            for l in range(2):
                sp.dma_start(sorted_rows[l][:, :], a["empty_rows"]).then_inc(RS[l]["fill"], 16)
            sp.wait_ge(a_av, 8 * BATCH)
            for dst, src in ((up0, a["up0"]), (gate0, a["gate0"])):
                sp.dma_start(dst, src).then_inc(ld_m0, 16)
            sp.wait_ge(i_h, 1)
            for dst, src in ((gate1, a["gate1"]), (down1, a["down1"])):
                sp.dma_start(dst, src).then_inc(ld_m1, 16)
            def tiles(l):
                q = RS[l]
                sp.wait_ge(q["dispatched"], 16 * TILES)

                def load(i, off):
                    k, r = i * RING + off, off % RING
                    if off >= RING:
                        sp.wait_ge(q["xk"], k - RING + 1)
                        sp.wait_ge(q["y"], k - RING + 1)
                        sp.wait_ge(q["sent"][r], (i + off // RING) * 16)
                    sp.dma_start(slot_in[:, r, :], sorted_rows[l][bass.ds(k * P, P), :]).then_inc(q["load"][r], 16)

                for k in range(RING):
                    load(0, k)
                with sp.Fori(0, SLOTS // RING - 1) as i:
                    for u in range(RING):
                        load(i, RING + u)
                for k in range(SLOTS // RING * RING, SLOTS):
                    load(0, k)

            def returned(l):
                q = RS[l]
                for r in range(RING):
                    sp.wait_ge(q["sent"][r], 16 * LOADS[r])
                with sp.Fori(0, NCH // 2) as i:
                    for k in range(2):
                        t = i * 2 + k
                        sp.wait_ge(q["back"], t + 1)
                        sp.dma_start(sqb[:, k, :].rearrange("p (n d) -> p n d", d=D),
                                     token_rows[l][bass.ds(t * CH, CH), :].rearrange("(n p) d -> p n d", p=P)
                                     ).then_inc(q["rows"][k], 16)

            tiles(0)
            sp.dma_start(up1, a["up1"]).then_inc(ld_m1, 16)
            returned(0)
            tiles(1)
            returned(1)
            with sp.Fori(0, NCH) as t:
                sp.wait_ge(RS[1]["x"], t + 3)
                sp.dma_start(a["out"][:, bass.ds(t * CH, CH)], X[:, bass.ds(t * CH, CH)]).then_inc(st_out, 16)
            sp.wait_ge(st_out, 16 * NCH)

        @block.tensor
        def _(pe):
            def ln(call, src):
                with pe.Fori(0, 2) as i:
                    for pair in range(2):
                        for k in (2 * pair, 2 * pair + 1):
                            t = 8 * call + i * 4 + k
                            pe.wait_ge(ln_xn, t + 1)
                            nc.tensor.matmul(PS[:, LN_PSC + k, :], center[:, :], src[:, bass.ds(i * 4 * CH + k * CH, CH)],
                                             start=True, stop=True).then_inc(ln_cen, 1)
                        for k in (2 * pair, 2 * pair + 1):
                            t = 8 * call + i * 4 + k
                            pe.wait_ge(ln_sq, t + 1)
                            pe.wait_ge(ln_lv, t + 1)
                            nc.tensor.matmul(PS[:, LN_PSV + k % 2, :], meanm[:, :], sqb[:, k, :],
                                             start=True, stop=True).then_inc(ln_var, 1)

            for l in range(2):
                for n in ("xt", "back"):
                    nc.tensor.sem_inc(RS[l][n], 2)
            pe.wait_ge(ld_c, 80)
            pe.wait_ge(mod_silu, 1)
            for l in range(2):
                for m in range(6):
                    c = (l * 6 + m) * BATCH
                    last = nc.tensor.matmul(PS[:, 7, c:c + BATCH], wmod[:, l, m * D:(m + 1) * D], sc[:, l, :],
                                            start=True, stop=True)
            last.then_inc(mod_ps, 1)

            pe.wait_ge(ld_x, 64)
            pe.wait_ge(credit, 2)
            ln(LN_MODA0, X)
            pe.wait_ge(ln_out, LNO + 8)
            ln(LN_ATTN, H)
            pe.wait_ge(ln_out, LNO + 16)
            pe.wait_ge(ld_a, 112)

            def scores(b, par, u):
                U = b * 8 + u
                j = u // 2
                r = slice(32 * j, 32 * j + 32)
                s = 2 * (u % 2)
                if u == 0:
                    pe.wait_ge(a_qsb, b + 1)
                for n in range(2):
                    g = 2 * (u % 2) + n
                    nc.tensor.matmul(PS[:, s, n * SEQ:(n + 1) * SEQ], qm[r, par, g, P:SEQ], kf[r, par, :],
                                     start=True, stop=False)
                    nc.tensor.matmul(PS[:, s, n * SEQ + P:(n + 1) * SEQ], identb[:, :], maskqk[:, :],
                                     start=False, stop=True)
                for n in range(2):
                    g = 2 * (u % 2) + n
                    nc.tensor.matmul(PS[:, s + 1, n * P:(n + 1) * P], qm[r, par, g, 0:P], kf[r, par, 0:P],
                                     start=True, stop=False)
                    last = nc.tensor.matmul(PS[:, s + 1, n * P:(n + 1) * P], identb[:, :], maskqk[:, :],
                                            start=False, stop=True)
                last.then_inc(a_s, 1)

            def transposes(U, ub):
                pe.wait_ge(a_p, U + 1)
                if not (type(U) is int and U == 0):
                    pe.wait_ge(a_ptd, U)
                    pe.wait_ge(a_pta, U)
                for n, k in enumerate((4, 0, 5, 2)):
                    nc.tensor.transpose(PS[:, A_PST, n * P:(n + 1) * P], pr[:, ub, k * P:(k + 1) * P], ident[:, :])
                for n, k in enumerate((1, 3)):
                    last = nc.tensor.transpose(PS[:, A_PST + 1, n * P:(n + 1) * P], pr[:, ub, k * P:(k + 1) * P],
                                               ident[:, :])
                last.then_inc(a_t, 1)

            def weigh(U, b, par, u):
                ub = u % 2
                pe.wait_ge(a_ptd, U + 1)
                pe.wait_ge(a_pta, U + 1)
                if u == 0:
                    pe.wait_ge(a_va, b + 1)
                    if not (type(b) is int and b == 0):
                        pe.wait_ge(a_on, b)
                j = u // 2
                half, c = 64 * (j % 2), SEQ * (j // 2)
                for n in range(2):
                    h = 2 * u + n
                    first, end = u % 2 == 0 and n == 0, u % 2 == 1 and n == 1
                    nc.tensor.matmul(PS[half:half + 64, A_PSO, c:c + SEQ], va[:, par, 0, h, :],
                                     pT[:, ub, 2 * n:2 * n + 2, :].rearrange("p n q -> p (n q)"), start=first, stop=False)
                    last = nc.tensor.matmul(PS[half:half + 64, A_PSO, c + P:c + SEQ], va[:, par, 1, h, :],
                                            pT[:, ub, 4 + n, :], start=False, stop=end)
                last.then_inc(a_av, 1)

            def out_project(b):
                pe.wait_ge(a_on, b + 1)
                if not (type(b) is int and b == BATCH - 1):
                    pe.wait_ge(a_va, b + 2)
                nc.tensor.matmul(PS[:, A_PSM, SEQ:2 * SEQ], wout[:, :], ao[:, :], start=True, stop=True).then_inc(a_pj, 1)

            def project_qk(b, par, first=False):
                pe.wait_ge(a_nb, b + 1)
                if not first:
                    pe.wait_ge(a_att, b - 1)
                nc.tensor.matmul(PS[:, A_PSM, 0:SEQ], wqkv[:, 0:D], nb[:, par, :], start=True, stop=True)
                nc.tensor.matmul(PS[:, A_PSM, SEQ:2 * SEQ], wqkv[:, D:2 * D], nb[:, par, :],
                                 start=True, stop=True).then_inc(a_qkps, 1)

            def project_v(b, par):
                pe.wait_ge(a_qsb, b + 1)
                for n in range(2):
                    last = nc.tensor.matmul(PS[:, A_PSM, n * D:(n + 1) * D], nb[:, par, n * P:(n + 1) * P],
                                            wqkv[:, 2 * D:3 * D], start=True, stop=True)
                last.then_inc(a_vps, 1)

            def batch(b, par, head, tail):
                for u in range(8):
                    U = b * 8 + u
                    scores(b, par, u)
                    if u >= 1 or head:
                        transposes(U - 1, (u + 1) % 2)
                    if u >= 2:
                        weigh(U - 2, b, par, u - 2)
                    elif head:
                        weigh(U - 2, b - 1, 1 - par, u + 6)
                    if u == 3 and head:
                        out_project(b - 1)
                    if u == 4 and tail:
                        project_qk(b + 1, 1 - par, first=(type(b) is int and b == 0))
                    if u == 6 and tail:
                        project_v(b + 1, 1 - par)

            project_qk(0, 0, first=True)
            project_v(0, 0)
            batch(0, 0, False, True)
            with pe.Fori(0, BATCH // 2 - 1) as i:
                batch(i * 2 + 1, 1, True, True)
                batch(i * 2 + 2, 0, True, True)
            batch(BATCH - 1, 1, True, False)
            U = 8 * BATCH - 1
            transposes(U, 1)
            weigh(U - 1, BATCH - 1, 1, 6)
            weigh(U, BATCH - 1, 1, 7)
            out_project(BATCH - 1)

            pe.wait_ge(a_h, BATCH)
            ln(LN_G1, H)
            pe.wait_ge(ln_out, LNO + 24)
            pe.wait_ge(ld_b, 80)
            for c in range(NCH):
                s = slice(c * CH, (c + 1) * CH)
                nc.tensor.matmul(PS[:, c, :], wctx[:, :], ATT[:, s], start=True, stop=False)
                nc.tensor.matmul(PS[:, c, :], wx[:, :], XS[:, s], start=False, stop=True).then_inc(i_p, 1)
            pe.wait_ge(i_w, 1)
            with pe.Fori(0, STEPS - 1) as n:
                for c in range(NCH):
                    pe.wait_ge(i_v, n * NCH + c + 5)
                    nc.tensor.matmul(PS[:, c, :], wxs[:, :], V[:, c * CH:(c + 1) * CH], start=False, stop=True,
                                     skip_group_check=True).then_inc(i_p, 1)
            pe.wait_ge(i_h, 1)

            ln(LN_G2, H)
            pe.wait_ge(ln_out, LNO + 32)
            with pe.Fori(0, NCH // 2) as i:
                for k in range(2):
                    t = i * 2 + k
                    for j in range(FF // P):
                        pe.wait_ge(f_g, t * 4 + j + 1)
                        nc.tensor.matmul(PS[:, j, :], w1[:, j * P:(j + 1) * P], N[:, bass.ds(t * CH, CH)],
                                         start=True, stop=True).then_inc(f_h, 1)
                    pe.wait_ge(f_hy, t + 1)
                    for j in range(FF // P):
                        pe.wait_ge(f_g, t * 4 + j + 5)
                        last = nc.tensor.matmul(PS[:, 4 + k, :], w2[:, j, :], sqb[:, j, :],
                                                start=(j == 0), stop=(j == FF // P - 1))
                    last.then_inc(f_y, 1)

            def moe(c):
                E, NH, HID, l = c["E"], c["NH"], c["HID"], c["l"]
                up, gate, down, q = c["up"], c["gate"], c["down"], RS[c["l"]]
                up_f = up.rearrange("p e h -> p (e h)")
                gate_f = gate.rearrange("p e h -> p (e h)")
                down_f = (down[:, :, :, :] if l == 0 else down).rearrange("p e j d -> p (e j d)")

                with pe.Fori(0, NCH // 2) as i:
                    for k in range(2):
                        t = i * 2 + k
                        x = xnb[:, k, :]
                        pe.wait_ge(q["staged"], t + 1)
                        pe.wait_ge(q["logits_sb"], t + 1)
                        for n in range(4):
                            last = nc.tensor.matmul(PS[:, 4 + k, n * 8:(n + 1) * 8], x[:, n * P:(n + 1) * P],
                                                    c["rw"][:, :], start=True, stop=True)
                        last.then_inc(q["logits"], 1)
                        pe.wait_ge(q["xt_sb"], t + 1)
                        for n in range(4):
                            last = nc.tensor.transpose(PS[:, 2 + k, n * P:(n + 1) * P], x[:, n * P:(n + 1) * P], ident[:, :])
                        last.then_inc(q["xt"], 1)
                pe.wait_ge(q["onehot"], 1)
                oh = onehot.rearrange("p t e -> p (t e)")
                nc.tensor.matmul(PS[:, 6, 0:256], before[:, :], oh, start=True, stop=True)
                nc.tensor.matmul(PS[:, 7, 0:256], ones[:, :], oh, start=True, stop=True).then_inc(q["counts"], 1)

                def shared_down(t, hb):
                    j = t * NH + hb
                    pe.wait_ge(q["s_hidden"], j + 3)
                    if hb == 0 and not (type(t) is int and t == 0):
                        pe.wait_ge(q["s_x"], t)
                    m = nc.tensor.matmul(PS[:, 4, :], down[:, E, hb, :], rsb[:, hb % 2, :], start=(hb == 0), stop=(hb == NH - 1))
                    if hb == NH - 1:
                        m.then_inc(q["s_sum"], 1)

                def shared(t, first):
                    x = N[:, bass.ds(t * CH, CH)]
                    for hb in range(NH):
                        j = t * NH + hb
                        pe.wait_ge(q["s_silu"], j + 1)
                        nc.tensor.matmul(PS[:, hb % 2, :], gate[:, E, hb * P:(hb + 1) * P], x, start=True, stop=True)
                        pe.wait_ge(q["s_hidden"], j + 1)
                        nc.tensor.matmul(PS[:, 2 + hb % 2, :], up[:, E, hb * P:(hb + 1) * P], x,
                                         start=True, stop=True).then_inc(q["s_up"], 1)
                        if hb:
                            shared_down(t, hb - 1)
                        elif not first:
                            shared_down(t - 1, NH - 1)

                pe.wait_ge(q["xt_sb"], NCH + 2)
                pe.wait_ge(q["logits_sb"], NCH + 2)
                shared(0, True)
                with pe.Fori(1, NCH) as t:
                    shared(t, False)
                shared_down(NCH - 1, NH - 1)

                def expert(k):
                    return pe.value_load(eid[0:1, bass.ds(k, 1)], min_val=0, max_val=c["cap"])

                def turn(i, off):
                    k, r = i * RING + off, off % RING
                    pe.wait_ge(q["load"][r], (i + off // RING + 1) * 16)
                    if off:
                        pe.wait_ge(q["xf"], k)
                    nc.tensor.transpose(PS[:, 7, 0:P], slot_in[:, r, 0:D], ident[:, :]).then_inc(q["xk"], 1)

                def gate_up(i, off):
                    k, b = i * RING + off, off % 2
                    e = expert(k)
                    pe.wait_ge(q["xf"], k + 1)
                    if off >= 2:
                        pe.wait_ge(q["silu"], k - 1)
                    nc.tensor.matmul(PS[:, b, 0:HID], xnb[:, b, 0:P], gate_f[:, bass.ds(e * HID, HID)], start=True, stop=True)
                    if off >= 2:
                        pe.wait_ge(q["hidden"], k - 1)
                    nc.tensor.matmul(PS[:, 2 + b, 0:HID], xnb[:, b, 0:P], up_f[:, bass.ds(e * HID, HID)],
                                     start=True, stop=True).then_inc(q["up"], 1)

                def turn_hidden(i, off):
                    k, b = i * RING + off, off % 2
                    pe.wait_ge(q["hidden"], k + 1)
                    if off >= 2:
                        pe.wait_ge(q["hf"], k - 1)
                    for n in range(NH):
                        last = nc.tensor.transpose(PS[:, 4 + b, n * P:(n + 1) * P], rsb[:, b, n * P:(n + 1) * P], ident[:, :])
                    last.then_inc(q["ht"], 1)

                def sum_down(i, off):
                    k, b = i * RING + off, off % 2
                    e = expert(k)
                    pe.wait_ge(q["hf"], k + 1)
                    if off >= 1:
                        pe.wait_ge(q["y"], k)
                    for n in range(NH):
                        last = nc.tensor.matmul(PS[:, 6, 0:D], rsb[:, 2 + b, n * P:(n + 1) * P],
                                                down_f[:, bass.ds(e * (NH * D) + n * D, D)], start=(n == 0), stop=(n == NH - 1))
                    last.then_inc(q["down"], 1)

                def slot(i, off):
                    if off < SLOTS:
                        gate_up(i, off)
                    if off < SLOTS - 1:
                        turn(i, off + 1)
                    if 1 <= off <= SLOTS:
                        turn_hidden(i, off - 1)
                    if off >= 2:
                        sum_down(i, off - 2)

                pe.wait_ge(q["pos"], 1)
                pe.wait_ge(q["s_x"], NCH)
                turn(0, 0)
                for k in range(3):
                    slot(0, k)
                with pe.Fori(0, LOOPED) as i:
                    for u in range(RING):
                        slot(i, 3 + u)
                for k in range(3 + LOOPED * RING, SLOTS + 2):
                    slot(0, k)

                with pe.Fori(0, NCH // 2) as i:
                    for k in range(2):
                        t = i * 2 + k
                        pe.wait_ge(q["rows"][k], i * 16 + 16)
                        pe.wait_ge(q["x"], t + 1)
                        for n in range(4):
                            last = nc.tensor.transpose(PS[:, k, n * P:(n + 1) * P], sqb[:, k, n * P:(n + 1) * P], ident[:, :])
                        last.then_inc(q["back"], 1)

            pe.wait_ge(f_x, NCH)
            ln(LN_MODB0, X)
            pe.wait_ge(ln_out, LNO + 40)
            pe.wait_ge(ld_m0, LD_M0)
            moe(MOE[0])

            pe.wait_ge(RS[0]["x"], NCH + 2)
            ln(LN_MODA1, X)
            pe.wait_ge(ln_out, LNO + 48)
            pe.wait_ge(ld_l1, 96)

            def project_zv(b, par):
                pe.wait_ge(b_nb, b + 1)
                if not (type(b) is int and b == 0):
                    pe.wait_ge(b_va, b)
                for n in range(2):
                    x = nb[:, par, n * P:(n + 1) * P]
                    nc.tensor.matmul(PS[:, 4, n * 40:(n + 1) * 40], x, wp[:, :], start=True, stop=True)
                    last = nc.tensor.matmul(PS[:, 4, (1 + n) * D:(2 + n) * D], x, wv1[:, :], start=True, stop=True)
                last.then_inc(b_zv, 1)

            def transpose_leaves(b):
                pe.wait_ge(b_lv, b + 1)
                if not (type(b) is int and b == 0):
                    pe.wait_ge(b_lw, b)
                for g in range(2):
                    for n in range(2):
                        h = n * HEADS1 + 4 * g
                        last = nc.tensor.transpose(PS[:, 5, g * SEQ + n * P:g * SEQ + (n + 1) * P],
                                                   levels[DEPTH][:, h:h + 4, :].rearrange("p h l -> p (h l)"), ident[:, :])
                last.then_inc(b_lt, 1)

            def prefix_sums(b, par):
                pe.wait_ge(b_lf, b + 1)
                nc.tensor.matmul(PS[:, 5, :], prefix[:, :], lf[:, par, :, :].rearrange("p g t -> p (g t)"),
                                 start=True, stop=True).then_inc(b_w, 1)

            def scores1(b, par, u):
                r = slice(32 * u, 32 * u + 32)
                s = 2 * (u % 2)
                if u == 0:
                    pe.wait_ge(b_lw, b + 1)
                for n in range(2):
                    o = n * SEQ
                    nc.tensor.matmul(PS[:, s, o:o + SEQ], lw[r, par, n, 0:P], lf[r, par, n, :], start=True, stop=False)
                    nc.tensor.matmul(PS[:, s, o:o + P], identb[:, :], maskkq[:, :], start=False, stop=True)
                for n in range(2):
                    o = n * P
                    nc.tensor.matmul(PS[:, s + 1, o:o + P], lw[r, par, n, P:SEQ], lf[r, par, n, P:SEQ],
                                     start=True, stop=False)
                    last = nc.tensor.matmul(PS[:, s + 1, o:o + P], identb[:, :], maskkq[:, :], start=False, stop=True)
                last.then_inc(b_s, 1)

            def weigh1(U, b, par, u):
                ub = u % 2
                pe.wait_ge(b_p, U + 1)
                if u == 0:
                    pe.wait_ge(b_va, b + 1)
                    if not (type(b) is int and b < 2):
                        pe.wait_ge(b_x, b - 1)
                for n in range(2):
                    h = u + 4 * n
                    j = h // 2
                    half, c = 64 * (j // 2), SEQ * (j % 2)
                    nc.tensor.matmul(PS[half:half + 64, B_PSO + par, c:c + SEQ], va1[:, par, 0, h, :],
                                     pT[:, ub, 2 * n:2 * n + 2, :].rearrange("p n q -> p (n q)"),
                                     start=(h % 2 == 0), stop=False)
                    last = nc.tensor.matmul(PS[half:half + 64, B_PSO + par, c + P:c + SEQ], va1[:, par, 1, h, :],
                                            pT[:, ub, 4 + n, :], start=False, stop=(h % 2 == 1))
                last.then_inc(b_av, 1)

            def out_project1(b, par):
                pe.wait_ge(b_on, b + 1)
                nc.tensor.matmul(PS[:, B_PSO + par, 0:SEQ], wo1[:, :], ao[:, :], start=True, stop=True).then_inc(b_pj, 1)

            def batch1(b, par, head, tail):
                for u in range(4):
                    U = b * 4 + u
                    scores1(b, par, u)
                    if u == 3 and tail:
                        prefix_sums(b + 1, 1 - par)
                    if u:
                        weigh1(U - 1, b, par, u - 1)
                    elif head:
                        weigh1(U - 1, b - 1, 1 - par, 3)
                    if u == 0 and tail:
                        project_zv(b + 1, 1 - par)
                    if u == 3 and head:
                        out_project1(b - 1, 1 - par)
                    if u == 2 and tail:
                        transpose_leaves(b + 1)

            project_zv(0, 0)
            transpose_leaves(0)
            prefix_sums(0, 0)
            batch1(0, 0, False, True)
            with pe.Fori(0, BATCH // 2 - 1) as i:
                batch1(i * 2 + 1, 1, True, True)
                batch1(i * 2 + 2, 0, True, True)
            batch1(BATCH - 1, 1, True, False)
            weigh1(4 * BATCH - 1, BATCH - 1, 1, 3)
            out_project1(BATCH - 1, 1)

            pe.wait_ge(b_x, BATCH)
            ln(LN_MODB1, X)
            pe.wait_ge(ln_out, LNO + 56)
            pe.wait_ge(ld_m1, 64)
            moe(MOE[1])

        @block.scalar
        def _(act):
            nc.scalar.sem_inc(ln_lv, 2)
            nc.scalar.sem_inc(f_g, 4)
            nc.scalar.sem_inc(credit, 1)
            for l in range(2):
                nc.scalar.sem_inc(RS[l]["xt_sb"], 2)
                nc.scalar.sem_inc(RS[l]["s_silu"], 2)
            act.wait_ge(ld_c, 80)
            nc.scalar.activation(sc[:, :, :], cT[:, :, :], ACT.Silu).then_inc(mod_silu, 1)

            def ln(call):
                with act.Fori(0, 2) as i:
                    for pair in range(2):
                        for k in (2 * pair, 2 * pair + 1):
                            t = 8 * call + i * 4 + k
                            act.wait_ge(ln_cen, t + 1)
                            nc.scalar.activation(sqb[:, k, :], PS[:, LN_PSC + k, :], ACT.Square).then_inc(ln_sq, 1)
                        for k in (2 * pair, 2 * pair + 1):
                            t = 8 * call + i * 4 + k
                            act.wait_ge(ln_var, t + 1)
                            nc.scalar.activation(rsb[:, k, :], PS[:, LN_PSV + k % 2, :], ACT.Ln,
                                                 bias=EPS).then_inc(ln_lv, 1)
                        for k in (2 * pair, 2 * pair + 1):
                            t = 8 * call + i * 4 + k
                            act.wait_ge(ln_lv, t + 3)
                            nc.scalar.activation(rsb[:, k, :], rsb[:, k, :], ACT.Exp, scale=-0.5).then_inc(ln_rs, 1)

            nc.scalar.preload_act_table_set(LN_EXP)
            ln(LN_MODA0)
            ln(LN_ATTN)

            act.wait_ge(ld_a, 112)

            def exps(U, u):
                ub, s = u % 2, 2 * (u % 2)
                act.wait_ge(a_mx, U + 1)
                for n in range(2):
                    nc.scalar.activation(pr[:, ub, n * SEQ:(n + 1) * SEQ], PS[:, s, n * SEQ:(n + 1) * SEQ], ACT.Exp,
                                         bias=mneg[:, ub, n:n + 1])
                for n in range(2):
                    last = nc.scalar.activation(pr[:, ub, (4 + n) * P:(5 + n) * P], PS[:, s + 1, n * P:(n + 1) * P],
                                                ACT.Exp, bias=mneg[:, ub, 2 + n:3 + n])
                last.then_inc(a_p, 1)

            def copy_transposed(U, ub):
                act.wait_ge(a_t, U + 1)
                nc.scalar.activation(pT[:, ub, 4:6, :], PS[:, A_PST + 1, 0:2 * P].rearrange("p (n k) -> p n k", n=2),
                                     ACT.Copy).then_inc(a_pta, 1)

            def invert_sums(b):
                act.wait_ge(a_av, 8 * b + 8)
                for j in range(4):
                    half, c = 64 * (j % 2), SEQ * (j // 2)
                    last = nc.scalar.activation(rec[32 * j:32 * j + 32, :], PS[half + 32:half + 64, A_PSO, c:c + SEQ], ACT.Ln)
                last.then_inc(a_ln, 1)
                act.wait_ge(a_ln, b + 1)
                nc.scalar.activation(rec[:, :], rec[:, :], ACT.Exp, scale=-1.0).then_inc(a_rec, 1)

            def add_bias(b):
                act.wait_ge(a_pj, b + 1)
                nc.scalar.activation(ATT[:, bass.ds(b * SEQ, SEQ)], PS[:, A_PSM, SEQ:2 * SEQ], ACT.Identity,
                                     bias=col(C_OUTB)).then_inc(a_att, 1)

            def batch(b, par, head, tail):
                for u in range(8):
                    U = b * 8 + u
                    if u == 2 and head:
                        invert_sums(b - 1)
                    if u >= 1 or head:
                        copy_transposed(U - 1, (u + 1) % 2)
                    exps(U, u)
                    if u == 3 and head:
                        add_bias(b - 1)

            batch(0, 0, False, True)
            with act.Fori(0, BATCH // 2 - 1) as i:
                batch(i * 2 + 1, 1, True, True)
                batch(i * 2 + 2, 0, True, True)
            batch(BATCH - 1, 1, True, False)
            copy_transposed(8 * BATCH - 1, 1)
            invert_sums(BATCH - 1)
            add_bias(BATCH - 1)

            ln(LN_G1)
            with act.Fori(0, STEPS) as n:
                for c in range(NCH):
                    t = n * NCH + c
                    act.wait_ge(i_p, t + 1)
                    act.wait_ge(i_d, t + 1)
                    nc.scalar.activation(sqb[:, c % 4, :], PS[:, c, :], ACT.Tanh, bias=col(C_INL)).then_inc(i_u, 1)

            nc.scalar.preload_act_table_set(LN_EXP)
            ln(LN_G2)
            with act.Fori(0, NCH // 2) as i:
                for k in range(2):
                    t = i * 2 + k
                    for j in range(FF // P):
                        act.wait_ge(f_h, t * 4 + j + 1)
                        if j == 0:
                            act.wait_ge(f_y, t + 1)
                        nc.scalar.activation(sqb[:, j, :], PS[:, j, :], ACT.Gelu, bias=b1c[:, j:j + 1]).then_inc(f_g, 1)

            def moe(c):
                NH, HID, l, q = c["NH"], c["HID"], c["l"], RS[c["l"]]
                act.wait_ge(ln_out, LNO + 8 * c["ln"] + 8)
                with act.Fori(0, NCH // 2) as i:
                    for k in range(2):
                        t = i * 2 + k
                        act.wait_ge(q["xt"], t + 3)
                        nc.scalar.activation(rows[l][:, bass.ds(t * 4, 4), 0:D], PS[:, 2 + k, :].rearrange("p (n d) -> p n d", d=D),
                                             ACT.Copy).then_inc(q["xt_sb"], 1)
                if l:
                    act.wait_ge(q["step"], 2)
                    nc.scalar.activation(expl, less, ACT.Exp).then_inc(q["exp"], 1)

                def shared(t):
                    for hb in range(NH):
                        j = t * NH + hb
                        act.wait_ge(q["s_up"], j + 1)
                        act.wait_ge(q["s_hidden"], j + 1)
                        nc.scalar.activation(sqb[:, hb % 2, :], PS[:, hb % 2, :], ACT.Silu).then_inc(q["s_silu"], 1)

                with act.Fori(0, NCH // 4) as i:
                    for k in range(4):
                        shared(i * 4 + k)

                def copy_x(i, off):
                    k, b = i * RING + off, off % 2
                    act.wait_ge(q["xk"], k + 1)
                    nc.scalar.activation(xnb[:, b, 0:P], PS[:, 7, 0:P], ACT.Copy).then_inc(q["xf"], 1)

                def silu(i, off):
                    k, b = i * RING + off, off % 2
                    act.wait_ge(q["up"], k + 1)
                    if off >= 2:
                        act.wait_ge(q["hidden"], k - 1)
                    nc.scalar.activation(sqb[:, b, 0:HID], PS[:, b, 0:HID], ACT.Silu).then_inc(q["silu"], 1)

                def weight(i, off):
                    k, r = i * RING + off, off % RING
                    act.wait_ge(q["down"], k + 1)
                    if off >= RING:
                        act.wait_ge(q["sent"][r], (i + off // RING) * 16)
                    nc.scalar.activation(slot_out[:, r, :], PS[:, 6, 0:D], ACT.Copy,
                                         scale=slot_in[:, r, D + 1:D + 2]).then_inc(q["y"], 1)

                def slot(i, off):
                    if off < SLOTS:
                        silu(i, off)
                    if off < SLOTS - 1:
                        copy_x(i, off + 1)
                    if off >= 2:
                        weight(i, off - 2)

                copy_x(0, 0)
                for k in range(3 + RING):
                    slot(0, k)
                with act.Fori(0, LOOPED - 1) as i:
                    for u in range(RING):
                        slot(i, 3 + RING + u)
                for k in range(3 + LOOPED * RING, SLOTS + 2):
                    slot(0, k)

            nc.scalar.preload_act_table_set(LN_EXP)
            ln(LN_MODB0)
            moe(MOE[0])
            nc.scalar.preload_act_table_set(LN_EXP)
            ln(LN_MODA1)

            def exp_z(b):
                act.wait_ge(b_z, b + 1)
                nc.scalar.activation(ez[:, :], zb[:, :], ACT.Exp, scale=-1.0).then_inc(b_ez, 1)

            def copy_sums(b, par):
                act.wait_ge(b_w, b + 1)
                nc.scalar.activation(lw[:, par, :, :].rearrange("p g t -> p (g t)"), PS[:, 5, :], ACT.Copy).then_inc(b_lw, 1)

            def exps1(U, u):
                ub, s = u % 2, 2 * (u % 2)
                act.wait_ge(b_s, U + 1)
                nc.scalar.activation(pT[:, ub, 0:4, :].rearrange("p n q -> p (n q)"), PS[:, s, :], ACT.Exp, scale=1.0 / DEPTH)
                nc.scalar.activation(pT[:, ub, 4:6, :].rearrange("p n q -> p (n q)"), PS[:, s + 1, 0:SEQ], ACT.Exp,
                                     scale=1.0 / DEPTH).then_inc(b_p, 1)

            def invert_sums1(b, par):
                act.wait_ge(b_av, 4 * b + 4)
                for j in range(4):
                    half, c = 64 * (j // 2), SEQ * (j % 2)
                    last = nc.scalar.activation(rec[32 * j:32 * j + 32, :], PS[half + 32:half + 64, B_PSO + par, c:c + SEQ], ACT.Ln)
                last.then_inc(b_ln, 1)
                act.wait_ge(b_ln, b + 1)
                nc.scalar.activation(rec[:, :], rec[:, :], ACT.Exp, scale=-1.0).then_inc(b_rec, 1)

            def batch1(b, par, head, tail):
                for u in range(4):
                    if u == 1 and head:
                        invert_sums1(b - 1, 1 - par)
                    exps1(b * 4 + u, u)
                    if u == 0 and tail:
                        exp_z(b + 1)
                    if u == 3 and tail:
                        copy_sums(b + 1, 1 - par)

            exp_z(0)
            copy_sums(0, 0)
            batch1(0, 0, False, True)
            with act.Fori(0, BATCH // 2 - 1) as i:
                batch1(i * 2 + 1, 1, True, True)
                batch1(i * 2 + 2, 0, True, True)
            batch1(BATCH - 1, 1, True, False)
            invert_sums1(BATCH - 1, 1)

            ln(LN_MODB1)
            moe(MOE[1])

        @block.vector
        def _(dve):
            nc.vector.sem_inc(ln_xn, 4)
            nc.vector.sem_inc(ln_out, LNO)
            nc.vector.sem_inc(i_v, 4)
            nc.vector.sem_inc(f_hy, 2)
            nc.vector.sem_inc(f_y, 1)
            nc.vector.sem_inc(i_x, NCH)
            for l in range(2):
                for n in ("logits_sb", "s_hidden", "x"):
                    nc.vector.sem_inc(RS[l][n], 2)
            nc.vector.sem_inc(credit, 1)

            dve.wait_ge(mod_ps, 1)
            nc.vector.tensor_copy(mod[:, :, :, :].rearrange("p l m b -> p (l m b)"), PS[:, 7, 0:12 * BATCH]).then_inc(mod_step, 1)
            dve.wait_ge(mod_step, 1)
            for l in range(2):
                for n, m in ((0, 2), (1, 5)):
                    nc.vector.tensor_scalar(gsg[:, 2 * l + n, :], mod[:, l, m, :], 0.0, 2.0, ALU.is_ge, ALU.mult)
                    nc.vector.scalar_tensor_tensor(out=gab[:, 2 * l + n, :], in0=mod[:, l, m, :], scalar=-1.0,
                                                   in1=mod[:, l, m, :], op0=ALU.mult, op1=ALU.max)
                for m in (1, 4):
                    last = nc.vector.tensor_scalar(mod[:, l, m, :], mod[:, l, m, :], 1.0, None, ALU.add)
            last.then_inc(mod_step, 1)
            dve.wait_ge(mod_step, 2)
            nc.vector.tensor_scalar(gab[:, :, :], gab[:, :, :], 0.25, None, ALU.max)
            nc.vector.tensor_scalar(gsg[:, :, :], gsg[:, :, :], -1.0, None, ALU.add).then_inc(mod_step, 1)
            dve.wait_ge(mod_step, 3)
            nc.vector.tensor_tensor(gab[:, :, :], gsg[:, :, :], gab[:, :, :], ALU.mult).then_inc(mod_step, 1)
            dve.wait_ge(mod_step, 4)

            def ln(call, dst, scale, shift):
                with dve.Fori(0, 2) as i:
                    for pair in range(2):
                        for k in (2 * pair, 2 * pair + 1):
                            t = 8 * call + i * 4 + k
                            dve.wait_ge(ln_rs, t + 1)
                            dve.wait_ge(ln_out, t + 1)
                            nc.vector.tensor_tensor(xnb[:, k, :], PS[:, LN_PSC + k, :], rsb[:, k, :],
                                                    ALU.mult).then_inc(ln_xn, 1)
                        for k in (2 * pair, 2 * pair + 1):
                            t = 8 * call + i * 4 + k
                            dve.wait_ge(ln_xn, t + 5)
                            if scale.shape[1] == 1:
                                last = nc.vector.tensor_scalar(dst[:, bass.ds(i * 4 * CH + k * CH, CH)], xnb[:, k, :],
                                                               scale, shift, ALU.mult, ALU.add)
                            else:
                                for b in range(BPC):
                                    c = i * 4 * BPC + k * BPC + b
                                    last = nc.vector.tensor_scalar(
                                        dst[:, bass.ds(c * SEQ, SEQ)], xnb[:, k, b * SEQ:(b + 1) * SEQ],
                                        scale[:, bass.ds(c, 1)], shift[:, bass.ds(c, 1)], ALU.mult, ALU.add)
                            last.then_inc(ln_out, 1)

            ln(LN_MODA0, H, mod[:, 0, 1, :], mod[:, 0, 0, :])
            ln(LN_ATTN, N, col(C_GA), col(C_BA))

            dve.wait_ge(ld_a, 112)

            def maxima(U, u):
                ub, s = u % 2, 2 * (u % 2)
                dve.wait_ge(a_s, U + 1)
                nc.vector.reduce_max(mneg[:, ub, 0:2], PS[:, s, :].rearrange("p (n k) -> p n k", n=2), AX_X, negate=True)
                nc.vector.reduce_max(mneg[:, ub, 2:4], PS[:, s + 1, 0:2 * P].rearrange("p (n k) -> p n k", n=2), AX_X,
                                     negate=True).then_inc(a_mx, 1)

            def copy_transposed(U, ub):
                dve.wait_ge(a_t, U + 1)
                nc.vector.tensor_copy(pT[:, ub, 0:4, :].rearrange("p n k -> p (n k)"), PS[:, A_PST, :]).then_inc(a_ptd, 1)

            def queries(b, par):
                dve.wait_ge(a_qkps, b + 1)
                for g in range(4):
                    nc.vector.tensor_scalar(qm[:, par, g, :], PS[:, A_PSM, 0:SEQ], col(C_QB), qmask[:, g:g + 1],
                                                   ALU.add, ALU.mult)
                nc.vector.tensor_scalar(kf[:, par, :], PS[:, A_PSM, SEQ:2 * SEQ], col(C_KB), None, ALU.add).then_inc(a_qsb, 1)

            def values(b, par):
                dve.wait_ge(a_vps, b + 1)
                for g in range(4):
                    last = nc.vector.tensor_tensor(
                        va[:, par, :, g::4, HD0 * g:HD0 * (g + 1)],
                        PS[:, A_PSM, 0:2 * D].rearrange("p (n h d) -> p n h d", n=2, d=HD0)[:, :, g::4, :],
                        vb[:, :, :].rearrange("p n (h d) -> p n h d", d=HD0)[:, :, g::4, :], ALU.add)
                last.then_inc(a_va, 1)

            def normalise(b):
                dve.wait_ge(a_rec, b + 1)
                for j in range(4):
                    half, c = 64 * (j % 2), SEQ * (j // 2)
                    last = nc.vector.tensor_tensor(ao[32 * j:32 * j + 32, :], PS[half:half + 32, A_PSO, c:c + SEQ],
                                                   rec[32 * j:32 * j + 32, :], ALU.mult)
                last.then_inc(a_on, 1)

            def batch(b, par, head, tail):
                for u in range(8):
                    U = b * 8 + u
                    maxima(U, u)
                    if u >= 1 or head:
                        copy_transposed(U - 1, (u + 1) % 2)
                    if u == 2 and head:
                        normalise(b - 1)
                    if u == 4 and tail:
                        queries(b + 1, 1 - par)
                    if u == 6 and tail:
                        values(b + 1, 1 - par)

            queries(0, 0)
            dve.wait_ge(va_ones, 5)
            values(0, 0)
            batch(0, 0, False, True)
            with dve.Fori(0, BATCH // 2 - 1) as i:
                batch(i * 2 + 1, 1, True, True)
                batch(i * 2 + 2, 0, True, True)
            batch(BATCH - 1, 1, True, False)
            copy_transposed(8 * BATCH - 1, 1)
            normalise(BATCH - 1)

            ln(LN_G1, XS, col(C_G1), col(C_B1))
            dve.wait_ge(ld_b, 80)
            nc.vector.tensor_scalar(wxs[:, :], wx[:, :], DT * DT, None, ALU.mult).then_inc(i_w, 1)
            dve.wait_ge(i_z, 1)
            with dve.Fori(0, STEPS) as n:
                def state(c):
                    s = slice(c * CH, (c + 1) * CH)
                    dve.wait_ge(i_v, n * NCH + c + 5)
                    nc.vector.scalar_tensor_tensor(out=XS[:, s], in0=V[:, s], scalar=DT * DT, in1=XS[:, s],
                                                   op0=ALU.mult, op1=ALU.add).then_inc(i_x, 1)
                for c in range(NCH):
                    s = slice(c * CH, (c + 1) * CH)
                    dve.wait_ge(i_d, n * NCH + c + 5)
                    nc.vector.scalar_tensor_tensor(out=V[:, s], in0=V[:, s], scalar=1.0 - DT, in1=rsb[:, c % 4, :],
                                                   op0=ALU.mult, op1=ALU.add).then_inc(i_v, 1)
                    if c:
                        state(c - 1)
                state(NCH - 1)

            dve.wait_ge(i_h, 1)
            ln(LN_G2, N, col(C_G2), col(C_B2))
            with dve.Fori(0, NCH // 2) as i:
                for k in range(2):
                    t = i * 2 + k
                    dve.wait_ge(f_y, t + 2)
                    nc.vector.scalar_tensor_tensor(out=H[:, bass.ds(t * CH, CH)], in0=PS[:, 4 + k, :], scalar=col(C_FB2),
                                                   in1=H[:, bass.ds(t * CH, CH)], op0=ALU.add, op1=ALU.add).then_inc(f_hy, 1)
                    dve.wait_ge(f_hy, t + 3)
                    for b in range(BPC):
                        c = t * BPC + b
                        last = nc.vector.scalar_tensor_tensor(
                            out=X[:, bass.ds(c * SEQ, SEQ)], in0=H[:, bass.ds(c * SEQ, SEQ)], scalar=gab[:, 0, bass.ds(c, 1)],
                            in1=X[:, bass.ds(c * SEQ, SEQ)], op0=ALU.mult, op1=ALU.add)
                    last.then_inc(f_x, 1)

            def moe(c):
                E, NH, HID, l, q = c["E"], c["NH"], c["HID"], c["l"], RS[c["l"]]
                with dve.Fori(0, NCH // 2) as i:
                    for k in range(2):
                        t = i * 2 + k
                        dve.wait_ge(q["logits"], t + 1)
                        nc.vector.tensor_copy(lgt[:, bass.ds(t * 4, 4), :],
                                              PS[:, 4 + k, 0:32].rearrange("p (n e) -> p n e", n=4)).then_inc(q["logits_sb"], 1)
                dve.wait_ge(q["logits_sb"], NCH + 2)

                done = [0]

                def link(ins):
                    done[0] += 1
                    ins.then_inc(q["step"], 1)
                    dve.wait_ge(q["step"], done[0])

                def over(x, shape):
                    return x.to_broadcast(shape)

                def last_axis(x):
                    return x.rearrange("p (n o) -> p n o", o=1)

                T8 = [P, TILES, 8]
                top, total, invert, weight, place_f = [small[:, n, 0:TILES] for n in range(5)]
                link(nc.vector.reduce_max(top, lgt, AX_X))
                link(nc.vector.tensor_tensor(less, lgt, over(last_axis(top), T8), ALU.subtract))
                link(nc.vector.tensor_scalar(cand, less, 0.0, None, ALU.is_equal))
                link(nc.vector.tensor_tensor(cand, cand, over(rank[:, :].rearrange("p (o e) -> p o e", o=1), T8), ALU.mult))
                link(nc.vector.reduce_max(top, cand, AX_X))
                nc.vector.tensor_tensor(onehot, cand, over(last_axis(top), T8), ALU.is_equal).then_inc(q["onehot"], 1)
                dve.wait_ge(q["onehot"], 1)
                if l:
                    dve.wait_ge(q["exp"], 1)
                    link(nc.vector.reduce_sum(total, expl, AX_X))
                    link(nc.vector.reciprocal(invert, total))
                    link(nc.vector.tensor_scalar(weight, onehot[:, :, 7], -ALPHA, ALPHA, ALU.mult, ALU.add))
                    dve.wait_ge(q["xt_sb"], NCH + 2)
                    link(nc.vector.tensor_tensor(rows[l][:, :, D + 1], weight, invert, ALU.mult))
                else:
                    dve.wait_ge(q["xt_sb"], NCH + 2)
                    link(nc.vector.memset(rows[l][:, :, D + 1], 1.0))
                link(nc.vector.tensor_copy(rows[l][:, :, D].bitcast(mybir.dt.int32), token_ids[:, :]))
                dve.wait_ge(q["counts"], 1)
                cnt = PS[:, 7, 0:256].rearrange("p (t e) -> p t e", e=8)
                cum = PS[:, 6, 0:256].rearrange("p (t e) -> p t e", e=8)
                link(nc.vector.tensor_copy(cnt_a, cnt))
                src, dst = cnt_a, cnt_b
                for n in (1, 2, 4, 8, 16):
                    nc.vector.tensor_copy(dst[:, 0:n, :], src[:, 0:n, :])
                    link(nc.vector.tensor_tensor(dst[:, n:, :], src[:, n:, :], src[:, 0:TILES - n, :], ALU.add))
                    src, dst = dst, src
                per = src[:, TILES - 1, :]
                tiles, ends, base = [small[:, n, 0:8] for n in (5, 6, 7)]
                gt = steps8.rearrange("p (e m) -> p e m", e=8)
                link(nc.vector.tensor_tensor(gt, over(last_axis(per), [P, 8, 40]),
                                             over(tile_starts[:, :].rearrange("p (o m) -> p o m", o=1), [P, 8, 40]), ALU.is_gt))
                link(nc.vector.reduce_sum(tiles, gt, AX_X))
                g8 = steps8[:, 0:64].rearrange("p (e f) -> p e f", e=8)
                link(nc.vector.tensor_tensor(g8, upto[:, :, :], over(tiles.rearrange("p (o f) -> p o f", o=1), [P, 8, 8]), ALU.mult))
                link(nc.vector.reduce_sum(ends, g8, AX_X))
                link(nc.vector.tensor_tensor(base, ends, tiles, ALU.subtract))
                link(nc.vector.tensor_scalar(base, base, float(P), None, ALU.mult))
                link(nc.vector.tensor_tensor(place, src, cum, ALU.add))
                link(nc.vector.tensor_tensor(place, place, cnt, ALU.subtract))
                link(nc.vector.tensor_tensor(place, place, over(base.rearrange("p (o f) -> p o f", o=1), T8), ALU.add))
                link(nc.vector.tensor_tensor(place, place, onehot, ALU.mult))
                link(nc.vector.reduce_sum(place_f, place, AX_X))
                link(nc.vector.tensor_copy(pos[:, :], place_f))
                ge = steps8.rearrange("p (m e) -> p m e", e=8)
                link(nc.vector.tensor_tensor(ge, over(last_axis(tile_ids[:, :]), [P, 40, 8]),
                                             over(ends.rearrange("p (o f) -> p o f", o=1), [P, 40, 8]), ALU.is_ge))
                link(nc.vector.reduce_sum(small[:, 0, :], ge, AX_X))
                nc.vector.tensor_scalar(eid[:, :], small[:, 0, :], float(c["cap"]), None, ALU.min).then_inc(q["pos"], 1)

                def hidden(t, hb):
                    j = t * NH + hb
                    dve.wait_ge(q["s_silu"], j + 3)
                    nc.vector.tensor_tensor(rsb[:, hb % 2, :], sqb[:, hb % 2, :], PS[:, 2 + hb % 2, :],
                                            ALU.mult).then_inc(q["s_hidden"], 1)

                def gated(t, ps):
                    for b in range(BPC):
                        n = t * BPC + b
                        last = nc.vector.scalar_tensor_tensor(
                            out=X[:, bass.ds(n * SEQ, SEQ)], in0=ps[:, b * SEQ:(b + 1) * SEQ],
                            scalar=gab[:, 2 * l + 1, bass.ds(n, 1)], in1=X[:, bass.ds(n * SEQ, SEQ)],
                            op0=ALU.mult, op1=ALU.add)
                    return last

                def add_shared(t):
                    dve.wait_ge(q["s_sum"], t + 1)
                    gated(t, PS[:, 4, :]).then_inc(q["s_x"], 1)

                for hb in range(NH):
                    hidden(0, hb)
                with dve.Fori(1, NCH) as t:
                    hidden(t, 0)
                    add_shared(t - 1)
                    for hb in range(1, NH):
                        hidden(t, hb)
                add_shared(NCH - 1)

                def gate_hidden(i, off):
                    k, b = i * RING + off, off % 2
                    dve.wait_ge(q["silu"], k + 1)
                    if off >= 2:
                        dve.wait_ge(q["ht"], k - 1)
                    nc.vector.tensor_tensor(rsb[:, b, 0:HID], sqb[:, b, 0:HID], PS[:, 2 + b, 0:HID],
                                            ALU.mult).then_inc(q["hidden"], 1)

                def copy_hidden(i, off):
                    k, b = i * RING + off, off % 2
                    dve.wait_ge(q["ht"], k + 1)
                    if off >= 2:
                        dve.wait_ge(q["down"], k - 1)
                    nc.vector.tensor_copy(rsb[:, 2 + b, 0:HID], PS[:, 4 + b, 0:HID]).then_inc(q["hf"], 1)

                def slot(i, off):
                    if off < SLOTS:
                        gate_hidden(i, off)
                    if 1 <= off <= SLOTS:
                        copy_hidden(i, off - 1)

                for k in range(3):
                    slot(0, k)
                with dve.Fori(0, LOOPED) as i:
                    for u in range(RING):
                        slot(i, 3 + u)
                for k in range(3 + LOOPED * RING, SLOTS + 2):
                    slot(0, k)

                with dve.Fori(0, NCH // 2) as i:
                    for k in range(2):
                        t = i * 2 + k
                        dve.wait_ge(q["back"], t + 3)
                        gated(t, PS[:, k, :]).then_inc(q["x"], 1)

            ln(LN_MODB0, N, mod[:, 0, 4, :], mod[:, 0, 3, :])
            dve.wait_ge(ld_m0, LD_M0)
            moe(MOE[0])
            dve.wait_ge(RS[0]["x"], NCH + 2)
            ln(LN_MODA1, N, mod[:, 1, 1, :], mod[:, 1, 0, :])

            dve.wait_ge(ld_l1, 96)

            def values1(b, par):
                dve.wait_ge(b_zv, b + 1)
                nc.vector.tensor_tensor(zb[:, :], PS[:, 4, 0:80], bp[:, :, :].rearrange("p n z -> p (n z)"), ALU.add).then_inc(b_z, 1)
                for g in range(2):
                    last = nc.vector.tensor_copy(
                        va1[:, par, :, g::2, HD1 * g:HD1 * (g + 1)],
                        PS[:, 4, D:3 * D].rearrange("p (n h d) -> p n h d", n=2, d=HD1)[:, :, g::2, :])
                last.then_inc(b_va, 1)

            def leaves(b):
                dve.wait_ge(b_ez, b + 1)
                L = b * 6
                nc.vector.tensor_scalar(ez[:, :], ez[:, :], 1.0, None, ALU.add).then_inc(b_st, 1)
                dve.wait_ge(b_st, L + 1)
                e = ez[:, :].rearrange("p (h d o) -> p h d o", d=DEPTH, o=1)
                nc.vector.reciprocal(pq[:, :, :, 0:1], e).then_inc(b_st, 1)
                dve.wait_ge(b_st, L + 2)
                nc.vector.tensor_scalar(pq[:, :, :, 1:2], pq[:, :, :, 0:1], -1.0, 1.0, ALU.mult, ALU.add).then_inc(b_st, 1)
                for d in range(2, DEPTH + 1):
                    dve.wait_ge(b_st, L + d + 1)
                    m = 2 ** (d - 1)
                    up = (pq[:, :, 0, :] if d == 2 else levels[d - 1][:, :, :]).rearrange("p h (m o) -> p h m o", o=1)
                    step = pq[:, :, d - 1:d, :]
                    last = nc.vector.tensor_tensor(levels[d][:, :, :].rearrange("p h (m o) -> p h m o", o=2),
                                                   up.to_broadcast([P, 2 * HEADS1, m, 2]),
                                                   step.to_broadcast([P, 2 * HEADS1, m, 2]), ALU.mult)
                    last.then_inc(b_lv if d == DEPTH else b_st, 1)

            def copy_leaves(b, par):
                dve.wait_ge(b_lt, b + 1)
                nc.vector.tensor_copy(lf[:, par, :, :].rearrange("p g t -> p (g t)"), PS[:, 5, :]).then_inc(b_lf, 1)

            def normalise1(b, par):
                dve.wait_ge(b_rec, b + 1)
                for j in range(4):
                    half, c = 64 * (j // 2), SEQ * (j % 2)
                    last = nc.vector.tensor_tensor(ao[32 * j:32 * j + 32, :], PS[half:half + 32, B_PSO + par, c:c + SEQ],
                                                   rec[32 * j:32 * j + 32, :], ALU.mult)
                last.then_inc(b_on, 1)

            def residual1(b, par):
                dve.wait_ge(b_pj, b + 1)
                s = bass.ds(b * SEQ, SEQ)
                nc.vector.scalar_tensor_tensor(out=X[:, s], in0=PS[:, B_PSO + par, 0:SEQ], scalar=gab[:, 2, bass.ds(b, 1)],
                                               in1=X[:, s], op0=ALU.mult, op1=ALU.add).then_inc(b_x, 1)

            def batch1(b, par, head, tail):
                if tail:
                    values1(b + 1, 1 - par)
                    leaves(b + 1)
                if head:
                    normalise1(b - 1, 1 - par)
                if tail:
                    copy_leaves(b + 1, 1 - par)
                if head:
                    residual1(b - 1, 1 - par)

            dve.wait_ge(va_ones, 8)
            values1(0, 0)
            leaves(0)
            copy_leaves(0, 0)
            batch1(0, 0, False, True)
            with dve.Fori(0, BATCH // 2 - 1) as i:
                batch1(i * 2 + 1, 1, True, True)
                batch1(i * 2 + 2, 0, True, True)
            batch1(BATCH - 1, 1, True, False)
            normalise1(BATCH - 1, 1)
            residual1(BATCH - 1, 1)

            dve.wait_ge(b_x, BATCH)
            ln(LN_MODB1, N, mod[:, 1, 4, :], mod[:, 1, 3, :])
            moe(MOE[1])

        @block.gpsimd
        def _(pool):
            nc.gpsimd.sem_inc(i_d, 4)

            def stage(b, par):
                if not (type(b) is int and b < 2):
                    pool.wait_ge(a_vps, b - 1)
                nc.gpsimd.tensor_copy(nb[:, par, :], N[:, bass.ds(b * SEQ, SEQ)]).then_inc(a_nb, 1)

            def residual(b):
                pool.wait_ge(a_att, b + 1)
                s = bass.ds(b * SEQ, SEQ)
                nc.gpsimd.tensor_tensor(H[:, s], H[:, s], ATT[:, s], ALU.add).then_inc(a_h, 1)

            def clear_values(x, count, width):
                nc.gpsimd.memset(x, 0.0).then_inc(va_ones, 1)
                for g in range(32 // width):
                    pool.wait_ge(va_ones, count + 1)
                    nc.gpsimd.memset(x[:, :, :, g::32 // width, 32 + width * g:32 + width * (g + 1)], 1.0).then_inc(va_ones, 1)

            clear_values(va, 0, HD0)
            pool.wait_ge(ln_out, LNO + 16)
            stage(0, 0)
            stage(1, 1)
            with pool.Fori(0, BATCH // 2 - 1) as i:
                for k in range(2):
                    stage(i * 2 + k + 2, k)
                    residual(i * 2 + k)
            residual(BATCH - 2)
            residual(BATCH - 1)

            pool.wait_ge(a_vps, BATCH)
            nc.gpsimd.memset(V[:, :], 0.0).then_inc(i_z, 1)
            pool.wait_ge(ln_out, LNO + 24)
            with pool.Fori(0, STEPS) as n:
                for c in range(NCH):
                    t = n * NCH + c
                    pool.wait_ge(i_u, t + 1)
                    pool.wait_ge(i_x, t + 1)
                    pool.wait_ge(i_v, t + 1)
                    nc.gpsimd.tensor_tensor(rsb[:, c % 4, :], sqb[:, c % 4, :], XS[:, c * CH:(c + 1) * CH],
                                            ALU.subtract).then_inc(i_d, 1)
            pool.wait_ge(i_x, NCH + STEPS * NCH)
            nc.gpsimd.tensor_tensor(H[:, 0:TOK], H[:, 0:TOK], XS[:, :], ALU.add).then_inc(i_h, 1)

            def moe(c):
                l, q = c["l"], RS[c["l"]]
                pool.wait_ge(ln_out, LNO + 8 * c["ln"] + 8)
                with pool.Fori(0, NCH // 2) as i:
                    for k in range(2):
                        t = i * 2 + k
                        pool.wait_ge(q["xt"], t + 1)
                        nc.gpsimd.tensor_copy(xnb[:, k, :], N[:, bass.ds(t * CH, CH)]).then_inc(q["staged"], 1)
                pool.wait_ge(q["pos"], 1)
                pool.wait_ge(q["fill"], 16)
                for n in range(TILES):
                    nc.gpsimd.indirect_dma_start(sorted_rows[l][:, :], bass.IndirectOffsetOnAxis(pos[:, n:n + 1], 0),
                                                 rows[l][:, n, :], None).then_inc(q["dispatched"], 16)

                def send(k):
                    r = k % RING
                    pool.wait_ge(q["y"], k + 1)
                    nc.gpsimd.indirect_dma_start(
                        token_rows[l][:, :], bass.IndirectOffsetOnAxis(slot_in[:, r, D:D + 1].bitcast(mybir.dt.int32), 0),
                        slot_out[:, r, :], None).then_inc(q["sent"][r], 16)

                for k in range(SLOTS):
                    send(k)

            moe(MOE[0])

            def stage1(b, par):
                if not (type(b) is int and b < 2):
                    pool.wait_ge(b_zv, b - 1)
                nc.gpsimd.tensor_copy(nb[:, par, :], N[:, bass.ds(b * SEQ, SEQ)]).then_inc(b_nb, 1)

            pool.wait_ge(RS[0]["x"], NCH + 2)
            clear_values(va1, 5, HD1)
            pool.wait_ge(ln_out, LNO + 48)
            stage1(0, 0)
            stage1(1, 1)
            with pool.Fori(0, BATCH // 2 - 1) as i:
                for k in range(2):
                    stage1(i * 2 + k + 2, k)
            moe(MOE[1])


def kernel(**inputs):
    import numpy as np
    import ml_dtypes
    import concourse.bacc as _bacc
    from concourse.bass_utils import run_bass_kernel_spmd as _run

    g = {k: np.asarray(v) for k, v in inputs.items()}
    f = np.float32
    nc = _bacc.Bacc("TRN2", target_bir_lowering=False, num_devices=1)
    arr = {}
    arr["xT"] = g["L0_attn_x"].reshape(TOK, D).T
    arr["cT"] = np.stack([g["L0_c"].T, g["L1_c"].T], 1)
    arr["wmod"] = np.stack([g["L0_wmod"], g["L1_wmod"]], 1)
    names = ["L0_attn_out_b", "L0_attn_g_attn", "L0_attn_b_attn", "L0_attn_g1", "L0_attn_b1", "L0_attn_g2",
             "L0_attn_b2", "L0_attn_b_inl", "L0_attn_ff_b2"]
    qb = g["L0_attn_qkv_b"].reshape(3, D)
    arr["cols"] = np.stack([qb[0], qb[1]] + [g[n] for n in names] + [np.zeros(D, f)] * 5, 1)
    arr["center"] = (np.eye(D) - 1.0 / D).astype(f)
    arr["meanm"] = np.full((D, D), 1.0 / D, f)
    arr["ident"] = np.eye(P, dtype=f)
    arr["identb"] = np.eye(P).astype(ml_dtypes.bfloat16)
    q, k = np.arange(P)[:, None], np.arange(P)[None, :]
    arr["maskqk"] = np.where(k > q, -1e30, 0.0).astype(ml_dtypes.bfloat16)
    arr["maskkq"] = np.where(k < q, -1e30, 0.0).astype(ml_dtypes.bfloat16)
    arr["qmask"] = np.where((np.arange(P)[:, None] % 32) // HD0 == np.arange(4)[None, :], HD0 ** -0.5, 0.0).astype(f)
    arr["vb"] = np.broadcast_to(qb[2], (P, 2, D))
    arr["wqkv"] = g["L0_attn_qkv_w"]
    arr["wout"] = g["L0_attn_out_w"]
    arr["wctx"] = g["L0_attn_w_ctx"]
    arr["wx"] = g["L0_attn_w_x"]
    arr["w1"] = g["L0_attn_ff_w1"]
    arr["w2"] = g["L0_attn_ff_w2"].reshape(FF // P, P, D).transpose(1, 0, 2)
    arr["b1c"] = g["L0_attn_ff_b1"].reshape(FF // P, P).T
    up = np.concatenate([g["L0_ffn_up"], g["L0_ffn_w_up_s"][None]], 0)
    gate = np.concatenate([g["L0_ffn_gate"], g["L0_ffn_w_gate_s"][None]], 0)
    down = np.concatenate([g["L0_ffn_down"], g["L0_ffn_w_down_s"][None]], 0)
    arr["up0"] = up.transpose(2, 0, 1)
    arr["gate0"] = gate.transpose(2, 0, 1)
    arr["down0"] = down.reshape(E0 + 1, D, HID0 // P, P).transpose(3, 0, 2, 1)
    arr["rw0"] = g["L0_ffn_router"].T
    up = np.concatenate([g["L1_ffn_up_w"], g["L1_ffn_shared_up_w"][None]], 0)
    gate = np.concatenate([g["L1_ffn_gate_w"], g["L1_ffn_shared_gate_w"][None]], 0)
    down = np.concatenate([g["L1_ffn_down_w"], g["L1_ffn_shared_down_w"][None]], 0)
    arr["up1"] = up.transpose(1, 0, 2)
    arr["gate1"] = gate.transpose(1, 0, 2)
    arr["down1"] = down.reshape(E1 + 1, HID1 // P, P, D).transpose(2, 0, 1, 3)
    arr["rw1"] = g["L1_ffn_router_w"]
    arr["wp"] = g["L1_attn_Wp"]
    arr["bp"] = np.broadcast_to(g["L1_attn_bp"], (P, 2, HEADS1 * DEPTH))
    arr["wv1"] = g["L1_attn_Wv"]
    arr["wo1"] = g["L1_attn_Wo"]
    x = np.arange(LEAVES)[:, None] ^ np.arange(LEAVES)[None, :]
    arr["prefix"] = np.kron(np.eye(SQ), np.sum([x < 2 ** n for n in range(DEPTH)], 0)).astype(f)
    arr["rank"] = np.broadcast_to(8.0 - np.arange(8), (P, 8)).astype(f)
    arr["before"] = np.triu(np.ones((P, P), f), 1)
    arr["ones"] = np.ones((P, P), f)
    arr["upto"] = np.broadcast_to(np.tril(np.ones((8, 8), f)), (P, 8, 8))
    arr["tile_starts"] = np.broadcast_to(np.arange(40) * P, (P, 40)).astype(f)
    arr["tile_ids"] = np.broadcast_to(np.arange(40), (P, 40)).astype(f)
    arr["token_ids"] = (np.arange(TILES)[None, :] * P + np.arange(P)[:, None]).astype(np.int32)
    empty = np.zeros((SLOTS * P, ROW), f)
    empty.view(np.int32)[:, D] = TOK + np.arange(SLOTS * P)
    arr["empty_rows"] = empty
    arrays, args = {}, {}
    for n, v in arr.items():
        v = np.ascontiguousarray(v)
        arrays[n + "_dram"] = v
        args[n] = nc.dram_tensor(n + "_dram", v.shape, mybir.dt.from_np(v.dtype), kind="ExternalInput").ap()
    args["out"] = nc.dram_tensor("out_dram", (D, TOK), FP32, kind="ExternalOutput").ap()
    adaln_kernel(nc, args)
    r = _run(nc, [arrays], core_ids=[0])
    return np.ascontiguousarray(r.results[0]["out_dram"].T).reshape(BATCH, SEQ, D)
```
